# Optimizing a Trainium2 kernel written in Bass

```python
import numpy as np
import jax
import jax.numpy as jnp

def _softmax(x, axis=-1):
    return jax.nn.softmax(x, axis=axis)

def _gelu(x):
    return jax.nn.gelu(x, approximate=True)

def _silu(x):
    return jax.nn.silu(x)

def _sigmoid(x):
    return jax.nn.sigmoid(x)

def _layernorm(x, axis=-1, eps=1e-05):
    m = jnp.mean(x, axis=axis, keepdims=True)
    v = jnp.var(x, axis=axis, keepdims=True)
    return (x - m) / jnp.sqrt(v + eps)

def _scatter_add(tgt, idx, src, axis=0):
    return tgt.at[idx].add(src)

def _segment_sum(src, seg, n):
    return jax.ops.segment_sum(src, seg, n)
kernel_name = 'mk_prb_d1_jaxref_r8_150ec5'

def setup_inputs(seed: int=0):
    np.random.seed(seed)
    _w = jnp.asarray

    def _L0_attn_setup():
        import jax, jax.numpy as jnp
        import numpy as np
        B, S, D, H = (2, 128, 128, 16)
        DK = D // H
        DE = D // 8
        SCALE = 1.0 / float(np.sqrt(DK))

        def _reference_tuple_inner(X, Wq, Wk, Wv, Wo, We):
            b, s, d = X.shape
            h, dk = (H, d // H)
            ctx = X @ We.T
            influence = jnp.einsum('bqe,bke->bqk', ctx, ctx)

            def heads(W):
                return (X @ W.T).reshape(b, s, h, dk).transpose(0, 2, 1, 3)
            Q, K, V = (heads(Wq), heads(Wk), heads(Wv))
            scores = jnp.einsum('bhqd,bhkd->bhqk', Q, K) * SCALE + 0.1 * influence[:, None]
            attn = jax.nn.softmax(scores, axis=-1)
            out = jnp.einsum('bhqk,bhkd->bhqd', attn, V)
            out = out.transpose(0, 2, 1, 3).reshape(b, s, d) @ Wo.T
            return (out, attn)
        key = jax.random.key(seed)
        ks = jax.random.split(key, 6)
        p = lambda k, shape: jax.random.normal(k, shape, dtype=jnp.float32) * 0.02
        return {'X': jax.random.normal(ks[0], (B, S, D), dtype=jnp.float32), 'Wq': p(ks[1], (D, D)), 'Wk': p(ks[2], (D, D)), 'Wv': p(ks[3], (D, D)), 'Wo': p(ks[4], (D, D)), 'We': p(ks[5], (DE, D))}
    _L0_attn_in = _L0_attn_setup()

    def _L0_ffn_setup():
        import jax, jax.numpy as jnp
        import numpy as np
        NUM_EXPERTS = 8
        TOP_K = 2
        key = jax.random.key(seed)
        ks = jax.random.split(key, 6)
        B, S, D, F = (2, 256, 128, 512)
        E = NUM_EXPERTS
        sd = 1.0 / np.sqrt(D)
        sf = 1.0 / np.sqrt(F)
        return {'x': jax.random.normal(ks[0], (B, S, D), dtype=jnp.float32), 'gate_w': jax.random.normal(ks[1], (E, D), dtype=jnp.float32) * sd, 'w1': jax.random.uniform(ks[2], (F, E, D), dtype=jnp.float32, minval=-sd, maxval=sd), 'b1': jax.random.uniform(ks[3], (E, F), dtype=jnp.float32, minval=-sd, maxval=sd), 'w2': jax.random.uniform(ks[4], (D, E, F), dtype=jnp.float32, minval=-sf, maxval=sf), 'b2': jax.random.uniform(ks[5], (E, D), dtype=jnp.float32, minval=-sf, maxval=sf)}
    _L0_ffn_in = _L0_ffn_setup()
    _d = {'L0_attn_X': _L0_attn_in['X'], 'L0_attn_Wq': _L0_attn_in['Wq'], 'L0_attn_Wk': _L0_attn_in['Wk'], 'L0_attn_Wv': _L0_attn_in['Wv'], 'L0_attn_Wo': _L0_attn_in['Wo'], 'L0_attn_We': _L0_attn_in['We'], 'L0_ffn_gate_w': _L0_ffn_in['gate_w'], 'L0_ffn_w1': _L0_ffn_in['w1'], 'L0_ffn_b1': _L0_ffn_in['b1'], 'L0_ffn_w2': _L0_ffn_in['w2'], 'L0_ffn_b2': _L0_ffn_in['b2']}
    _x0 = _d['L0_attn_X']
    _d['L0_attn_X'] = jax.random.normal(jax.random.fold_in(jax.random.key(seed), 1), (32, 256, 128), dtype=_x0.dtype)
    del _x0
    return _d

def reference(L0_attn_X, L0_attn_Wq, L0_attn_Wk, L0_attn_Wv, L0_attn_Wo, L0_attn_We, L0_ffn_gate_w, L0_ffn_w1, L0_ffn_b1, L0_ffn_w2, L0_ffn_b2):

    def _L0_attn_ref(X, Wq, Wk, Wv, Wo, We):
        import jax, jax.numpy as jnp
        import numpy as np
        B, S, D, H = (2, 128, 128, 16)
        DK = D // H
        DE = D // 8
        SCALE = 1.0 / float(np.sqrt(DK))

        def _reference_tuple_inner(X, Wq, Wk, Wv, Wo, We):
            b, s, d = X.shape
            h, dk = (H, d // H)
            ctx = X @ We.T
            influence = jnp.einsum('bqe,bke->bqk', ctx, ctx)

            def heads(W):
                return (X @ W.T).reshape(b, s, h, dk).transpose(0, 2, 1, 3)
            Q, K, V = (heads(Wq), heads(Wk), heads(Wv))
            scores = jnp.einsum('bhqd,bhkd->bhqk', Q, K) * SCALE + 0.1 * influence[:, None]
            attn = jax.nn.softmax(scores, axis=-1)
            out = jnp.einsum('bhqk,bhkd->bhqd', attn, V)
            out = out.transpose(0, 2, 1, 3).reshape(b, s, d) @ Wo.T
            return (out, attn)
        return _reference_tuple_inner(X, Wq, Wk, Wv, Wo, We)[0]

    def _L0_ffn_ref(x, gate_w, w1, b1, w2, b2):
        import jax, jax.numpy as jnp
        import numpy as np
        NUM_EXPERTS = 8
        TOP_K = 2
        logits = jnp.einsum('bsd,ed->bse', x, gate_w)
        probs = jax.nn.softmax(logits, axis=-1)
        topk_probs, topk_idx = jax.lax.top_k(probs, TOP_K)
        oh = jax.nn.one_hot(topk_idx, NUM_EXPERTS, dtype=x.dtype)
        h = jnp.einsum('bsd,fed,bske->bskf', x, w1, oh)
        h = h + jnp.take(b1, topk_idx, axis=0)
        h = jax.nn.gelu(h)
        y = jnp.einsum('bskf,def,bske->bskd', h, w2, oh)
        y = y + jnp.take(b2, topk_idx, axis=0)
        out = jnp.sum(y * topk_probs[..., None], axis=-2)
        return out
    x = L0_attn_X
    xn = _layernorm(x, axis=-1)
    x = x + _L0_attn_ref(xn, L0_attn_Wq, L0_attn_Wk, L0_attn_Wv, L0_attn_Wo, L0_attn_We) + _L0_ffn_ref(xn, L0_ffn_gate_w, L0_ffn_w1, L0_ffn_b1, L0_ffn_w2, L0_ffn_b2)
    return x

_drawn_inputs = setup_inputs


def setup_inputs(seed=0):
    import zlib

    import numpy as np

    out = dict(_drawn_inputs(seed))
    spreads = {}
    factors = {'L0_attn_Wq': 8.0,
     'L0_attn_Wk': 8.0,
     'L0_attn_Wv': 8.0,
     'L0_attn_Wo': 8.0,
     'L0_attn_We': 8.0,
     'L0_ffn_b1': 6.983,
     'L0_ffn_b2': 4.924}
    for name, (base, spread) in spreads.items():
        noise = np.random.default_rng([zlib.crc32(name.encode()), seed]).standard_normal(out[name].shape)
        drawn = base * np.exp(spread * noise) if base else spread * noise
        out[name] = jnp.asarray(drawn.astype(out[name].dtype))
    for name, factor in factors.items():
        out[name] = (out[name] * factor).astype(out[name].dtype)
    return out
```

```python
from contextlib import ExitStack

import concourse.bass as bass
from concourse import mybir

F32 = mybir.dt.float32
F16 = mybir.dt.float16
I32 = mybir.dt.int32
U32 = mybir.dt.uint32
ALU = mybir.AluOpType
ACT = mybir.ActivationFunctionType
AX = mybir.AxisListType

P = 128
D = 128
B = 32
S = 256
H = 16
DK = D // H
DE = D // 8
NE = 8
FF = 512
FC = FF // P
NT = B * S // P
EPS = 1e-5
SLOT = 256
ET = -(-(2 * B * S) // SLOT) + NE
ROWS = 3 * DK + 3 * DE
WS = 2.0 ** 8
FS = 2.0 ** 10
SCALE = DK ** -0.5
CTX = (0.1 / SCALE) ** 0.5
HALF = B // 2
NW = 3 * D + DE + NE
CQ, CK, CV, CE, CG = 0, D, 2 * D, 3 * D, 3 * D + DE
TERMS = ((0, 0), (0, 1), (1, 0))


class Step:

    def __init__(self, half, r):
        self.half, self.r = half, r

    def at(self, off):
        n = self.r + off
        return 2 * self.half + n, n % 2, self.half + n // 2


def attention_flags(k, b0):
    return {s: b0 <= k + off < b0 + HALF for s, off in (("p", 2), ("m", 1), ("x", 0), ("o", -1))}


ALL = dict.fromkeys("pmxo", True)


def attention_steps(eng, b0, body):
    for k in range(b0 - 2, b0 + 2):
        body(Step(k // 2, k % 2), attention_flags(k, b0), k)
    with eng.Fori(b0 // 2 + 1, b0 // 2 + HALF // 2 - 1, 1) as half:
        for r in range(2):
            body(Step(half, r), ALL, None)
    for k in range(b0 + HALF - 2, b0 + HALF + 1):
        body(Step(k // 2, k % 2), attention_flags(k, b0), k)


def expert_steps(eng, body):
    last = 1 + 4 * ((ET - 3) // 4)
    for t in range(-1, 5):
        body(t // 4, t % 4, t + 1 < ET, t >= 0, t >= 1)
    with eng.Fori(1, (last - 1) // 4, 1) as quad:
        for r in range(1, 5):
            body(quad, r, True, True, True)
    for t in range(last, ET + 1):
        body(t // 4, t % 4, t + 1 < ET, t < ET, True)


def build(nc, X, Wsmall, Wo, W1, W2, B1, B2, out):
    with ExitStack() as ctx:
        def sb(name, shape, dt):
            return ctx.enter_context(nc.sbuf_tensor(name, shape, dt))

        def sem(name):
            return ctx.enter_context(nc.semaphore(name))

        slots_x = nc.dram_tensor("slots_x", [ET * SLOT, 2 * D], F16, kind="Internal").ap()
        slots_y = nc.dram_tensor("slots_y", [ET * SLOT, D], F32, kind="Internal").ap()
        qk_dram = nc.dram_tensor("qk_dram", [2, 2, 2 * DK, H * S], F16, kind="Internal").ap()
        ctx_dram = nc.dram_tensor("ctx_dram", [2, 2 * DE, S], F16, kind="Internal").ap()

        x = sb("x", [P, NT, D], F32)
        rows = sb("rows", [P, NT, 2 * D], F16)
        xT = sb("xT", [P, 2, B * S], F16)
        w1 = sb("w1", [P, 2, NE * FF], F16)
        w2 = sb("w2", [P, 2, NE * FF], F16)
        ws = sb("ws", [P, 2, NW], F16)
        wo = sb("wo", [P, D], F32)
        b1 = sb("b1", [P, NE * FC], F32)
        b2 = sb("b2", [P, NE * D], F32)
        stack = sb("stack", [P, 2, 2, H, S], F16)
        A = sb("A", [P, 4, 2, S], F32)
        V = sb("V", [P, 2, 2, H, 32], F32)
        O = sb("O", [P, 2, 4, S], F32)
        hi_qk = sb("hi_qk", [P, 2, S], F16)
        lo_qk = sb("lo_qk", [P, 2, S], F16)
        part_c = sb("part_c", [DE, 2, S], F16)
        mx = sb("mx", [P, 2, 2, H], F32)
        negm = sb("negm", [P, 2, 2, 8], F16)
        mT = sb("mT", [8, 2, 2, P], F16)
        rden = sb("rden", [P, 2, H], F32)
        o_n = sb("o_n", [P, 2, H, DK], F32)
        oT = sb("oT", [P, 2 * P], F32)
        ident = sb("ident", [P, P], F32)
        ident16 = sb("ident16", [P, P], F16)
        before = sb("before", [P, P], F16)
        ones16 = sb("ones16", [P, P], F16)
        zeros = sb("zeros", [P, 2 * D], F16)
        stats = sb("stats", [P, NT, 6], F32)
        mean = sb("mean", [P, NT], F32)
        rstd = sb("rstd", [P, NT], F32)
        tmp = [sb(f"tmp{i}", [P, NT], F32) for i in range(4)]
        sel1 = sb("sel1", [P, NT, NE], F32)
        prob = [sb(f"prob{i}", [P, NT], F32) for i in range(2)]
        pos = [sb(f"pos{i}", [P, NT], U32) for i in range(2)]
        picked = sb("picked", [P, NT * NE], F16)
        cnt8 = sb("cnt8", [P, 4, NE], F32)
        cnt8i = sb("cnt8i", [P, NE], I32)
        tile_no = sb("tile_no", [1, ET], I32)
        tile_e = sb("tile_e", [1, 2, ET], I32)

        w_stage = stack[:, :, :, :, :].rearrange("p a b h s -> p (a b h s)").bitcast(F32)
        ws_stage = O[:, 0, :, :].rearrange("p g s -> p (g s)")[:, 0:NW]
        wins = O[:, :, :, :].rearrange("p a g s -> p (a g s)").bitcast(F16).rearrange("p (a n) -> p a n", a=NE)
        r_view = [A[:, i, :, :].rearrange("p a (b e) -> p (a b) e", e=NE) for i in range(4)]
        xn32 = V[:, 0, 0, :, :].rearrange("p h d -> p (h d)").rearrange("p (j d) -> p j d", d=D)
        v_view = [V[:, i // 2, i % 2, :, :].rearrange("p h (a e) -> p (h a) e", e=NE) for i in range(4)]
        scan, sel = v_view[1:3], [v_view[3], sel1[:, :, :]]
        tile_f = A[0:1, 0:2, :, :].rearrange("p b a s -> p (b a s)")
        free = rows[:, :, :].rearrange("p t d -> p (t d)")
        at = [0]

        def carve(n, dt):
            v = free[:, at[0]:at[0] + n * (2 if dt == F32 else 1)]
            at[0] += n * (2 if dt == F32 else 1)
            return v.bitcast(F32) if dt == F32 else v

        xr = [carve(2 * 2 * D, F16).rearrange("p (s c) -> p s c", s=2) for _ in range(4)]
        xt = [carve(2 * SLOT, F16).rearrange("p (a s) -> p a s", a=2) for _ in range(2)]
        h32 = [carve(FC * SLOT, F32).rearrange("p (f s) -> p f s", f=FC) for _ in range(2)]
        hp = [carve(2 * FC * SLOT, F16).rearrange("p (a f s) -> p a f s", a=2, f=FC) for _ in range(2)]
        ye = [carve(2 * D, F32).rearrange("p (s d) -> p s d", s=2) for _ in range(2)]
        y_tok = [carve(8 * D, F32).rearrange("p (j d) -> p j d", j=8) for _ in range(2)]
        assert at[0] <= NT * 2 * D

        bank = [ctx.enter_context(nc.psum_tensor(f"bank{i}", [P, 512], F32)) for i in range(8)]
        MX, EX, PV, MISC = bank[0:2], bank[2:4], bank[4:6], bank[6:8]

        s_x, s_small, s_w1, s_w2 = sem("s_x"), sem("s_small"), sem("s_w1"), sem("s_w2")
        s_const, s_zero, s_post = sem("s_const"), sem("s_zero"), sem("s_post")
        s_hiw, s_low = sem("s_hiw"), sem("s_low")
        s_d, s_sd, s_rows, s_tr, s_xt, s_gate = (sem(n) for n in ("s_d", "s_sd", "s_rows", "s_tr", "s_xt", "s_gate"))
        s_sub, s_exp8, s_m, s_cnt, s_routed, s_scat = (sem(n) for n in ("s_sub", "s_exp8", "s_m", "s_cnt", "s_routed", "s_scat"))
        s_qk, s_hq, s_lq, s_cx, s_ch, s_cl, s_v, s_vc = (sem(n) for n in ("s_qk", "s_hq", "s_lq", "s_cx", "s_ch", "s_cl", "s_v", "s_vc"))
        s_wr = [sem(f"s_wr{i}") for i in range(2)]
        s_st = [[sem(f"s_st{i}_{g}") for g in range(4)] for i in range(2)]
        s_mr = [[sem(f"s_mr{i}_{a}") for a in range(2)] for i in range(2)]
        s_mx, s_red, s_nm, s_mt, s_mte = (sem(n) for n in ("s_mx", "s_red", "s_nm", "s_mt", "s_mte"))
        s_ex, s_xp, s_pv, s_pe = (sem(n) for n in ("s_ex", "s_xp", "s_pv", "s_pe"))
        s_ot, s_rd, s_on, s_oT, s_oTe, s_wo, s_acc = (sem(n) for n in ("s_ot", "s_rd", "s_on", "s_oT", "s_oTe", "s_wo", "s_acc"))
        s_xr = [sem(f"s_xr{i}") for i in range(4)]
        s_ft, s_fx, s_fu, s_fg, s_fh, s_fl, s_fd, s_fy = (sem(n) for n in ("s_ft", "s_fx", "s_fu", "s_fg", "s_fh", "s_fl", "s_fd", "s_fy"))
        s_ys = [sem(f"s_ys{i}") for i in range(2)]
        s_yg = [sem(f"s_yg{i}") for i in range(2)]
        s_c1, s_cb, s_out = sem("s_c1"), sem("s_cb"), sem("s_out")

        block = ctx.enter_context(nc.Block())
        NCONST, NPOST = 10, 4

        def stage_off(s, off):
            n = s.r + off
            return n % 2

        @block.sync
        def _(sp):
            sp.dma_start(x[:, :, :], X.rearrange("(t p) d -> p t d", p=P)).then_inc(s_x, 16)
            sp.dma_start(ws_stage, Wsmall).then_inc(s_small, 16)
            sp.dma_start(wo[:, :], Wo).then_inc(s_small, 16)
            sp.dma_start(b1[:, :], B1).then_inc(s_small, 16)
            sp.dma_start(b2[:, :], B2.to_broadcast([P, NE * D])).then_inc(s_small, 16)
            sp.dma_start(w_stage[:, 0:NE * FF], W1).then_inc(s_w1, 16)
            sp.dma_start(w_stage[:, NE * FF:2 * NE * FF], W2).then_inc(s_w2, 16)
            sp.wait_ge(s_const, NCONST)
            zero_rows = slots_x.rearrange("(n p) c -> p n c", p=P)
            sp.dma_start(zero_rows, zeros[:, :].unsqueeze(1).to_broadcast([P, ET * SLOT // P, 2 * D])).then_inc(s_zero, 16)
            sp.wait_ge(s_post, NPOST)

            def attend(s, f, k):
                b, par, half = s.at(0)
                if f["x"]:
                    sp.wait_ge(s_mte, 2 * b + 2)
                    sp.dma_start(stack[ROWS:ROWS + 1, par, 0, 8:16, :], mT[:, 1, :, :].rearrange("h q t -> h (q t)")).then_inc(s_mr[par][1], 16)
                if f["p"]:
                    b2_, par2, half2 = s.at(2)
                    sp.wait_ge(s_lq, b2_ + 1)
                    if k is None or b2_ >= 2:
                        for g in range(4):
                            sp.wait_ge(s_st[par2][g], 128 * half2)
                    for side in range(2):
                        for part, src in enumerate((hi_qk, lo_qk)):
                            dst = qk_dram[par2, side, part * DK:(part + 1) * DK, :].rearrange("d (h t) -> h d t", t=S)
                            sp.dma_start(dst, src[:, side, :]).then_inc(s_wr[par2], 16)
                    sp.wait_ge(s_cl, b2_ + 1)
                    sp.dma_start(ctx_dram[par2].rearrange("(a c) t -> c a t", a=2), part_c[:, :, :]).then_inc(s_wr[par2], 16)
                    sp.wait_ge(s_wr[par2], 80 * (half2 + 1))
                for g in range(4):
                    if f["p"]:
                        if k is None or k >= 0:
                            sp.wait_ge(s_ex, 16 * b + 4 * g + 4)
                        hs = slice(4 * g * S, (4 * g + 4) * S)
                        for side, cut, first in ((0, 2 * DK, True), (1, DK, False)):
                            q = qk_dram[par2, side]
                            st = stack[:, par2, side, 4 * g:4 * g + 4, :]
                            two, one = (q[0:2 * DK, hs], q[0:DK, hs])
                            a, c = (two, one) if first else (one, two)
                            sp.dma_start(st[0:cut], a.rearrange("r (h t) -> r h t", t=S)).then_inc(s_st[par2][g], 16)
                            sp.dma_start(st[cut:3 * DK], c.rearrange("r (h t) -> r h t", t=S)).then_inc(s_st[par2][g], 16)
                            ctwo, cone = ctx_dram[par2], ctx_dram[par2, 0:DE]
                            a, c = (ctwo, cone) if first else (cone, ctwo)
                            n = a.shape[0]
                            sp.dma_start(st[3 * DK:3 * DK + n], a.unsqueeze(1).to_broadcast([n, 4, S])).then_inc(s_st[par2][g], 16)
                            sp.dma_start(st[3 * DK + n:ROWS], c.unsqueeze(1).to_broadcast([3 * DE - n, 4, S])).then_inc(s_st[par2][g], 16)
                    if g == 2 and f["m"]:
                        b1_, par1, _ = s.at(1)
                        sp.wait_ge(s_mte, 2 * b1_ + 1)
                        sp.dma_start(stack[ROWS:ROWS + 1, par1, 0, 0:8, :], mT[:, 0, :, :].rearrange("h q t -> h (q t)")).then_inc(s_mr[par1][0], 16)

            attention_steps(sp, 0, attend)

            xs = slots_x.rearrange("(n s p) c -> n p s c", s=2, p=P)
            ys = slots_y.rearrange("(n s p) d -> n p s d", s=2, p=P)
            sp.wait_ge(s_scat, 16 * 2 * NT)

            def expert(quad, r, a, b, c):
                t = 4 * quad + r
                if a:
                    todo = [(quad + (r + 3) // 4, (r + 3) % 4)]
                    if isinstance(quad, int):
                        todo = [(n // 4, n % 4) for n in ((0, 1, 2) if t < 0 else (t + 3,)) if n < ET]
                    for q2, r2 in todo:
                        n = 4 * q2 + r2
                        if not isinstance(n, int) or n >= 4:
                            sp.wait_ge(s_ft, n - 3)
                        if isinstance(n, int):
                            src = xs[n]
                        else:
                            src = xs[bass.ds(n, 1)].rearrange("n p s c -> (n p) s c")
                        sp.dma_start(xr[r2], src).then_inc(s_xr[r2], 16)
                if c:
                    n = t - 1
                    sp.wait_ge(s_fy, n + 1)
                    dst = ys[n] if isinstance(n, int) else ys[bass.ds(n, 1)].rearrange("n p s d -> (n p) s d")
                    sp.dma_start(dst, ye[(r - 1) % 2]).then_inc(s_ys[(r - 1) % 2], 16)

            expert_steps(sp, expert)

            out_v = out.rearrange("(n s p) d -> n p s d", s=2, p=P)

            def attend_store(s, f, k):
                attend(s, f, k)
                if f["o"]:
                    b = s.at(-1)[0]
                    sp.wait_ge(s_cb, b - HALF + 1)
                    for n in (b - HALF, b):
                        if isinstance(n, int):
                            sp.dma_start(out_v[n], x[:, 2 * n:2 * n + 2, :]).then_inc(s_out, 16)
                        else:
                            sp.dma_start(out_v[bass.ds(n, 1)].rearrange("n p s d -> (n p) s d"), x[:, bass.ds(2 * n, 2), :]).then_inc(s_out, 16)

            attention_steps(sp, HALF, attend_store)
            sp.wait_ge(s_out, 16 * B)

        @block.gpsimd
        def _(pool):
            c = [0]

            def const(ins, wait=False):
                c[0] += 1
                ins.then_inc(s_const, 1)
                if wait:
                    pool.wait_ge(s_const, c[0])

            const(pool.memset(zeros[:, :], 0.0))
            const(pool.memset(ident[:, :], 0.0))
            const(pool.memset(ident16[:, :], 0.0))
            const(pool.memset(before[:, :], 1.0))
            const(pool.memset(ones16[:, :], 1.0), wait=True)
            for m in (ident, ident16):
                const(pool.affine_select(out=m[:, :], in_=m[:, :], compare_op=ALU.not_equal, fill=1.0, base=0,
                                         pattern=[[-1, P]], channel_multiplier=1))
            const(pool.affine_select(out=before[:, :], in_=before[:, :], compare_op=ALU.is_gt, fill=0.0, base=0,
                                     pattern=[[1, P]], channel_multiplier=-1))
            const(pool.iota(tile_no[:, :], pattern=[[1, ET]], base=0, channel_multiplier=0))
            const(pool.memset(cnt8[:, 3, :], 0.0), wait=True)
            assert c[0] == NCONST
            pool.wait_ge(s_low, 3)
            pool.wait_ge(s_routed, 1)
            for par in range(2):
                pool.memset(stack[64:ROWS + 1, par, 1, :, :], 1.0).then_inc(s_post, 1)
                pool.wait_ge(s_post, par + 1)
            pool.memset(V[:, :, :, :, :], 0.0).then_inc(s_post, 1)
            pool.wait_ge(s_post, 3)
            pool.memset(V[:, :, :, :, DK:DK + 1], 1.0).then_inc(s_post, 1)
            pool.wait_ge(s_zero, 16)
            for t in range(NT):
                for j in range(2):
                    pool.indirect_dma_start(slots_x, bass.IndirectOffsetOnAxis(pos[j][:, t:t + 1], 0), rows[:, t, :], None).then_inc(s_scat, 16)
            for par in range(2):
                pool.wait_ge(s_ys[par], 16 * (ET // 2))
            for k in range(HALF + 1, B + 1):
                n = k - HALF - 1
                if n >= 2:
                    pool.wait_ge(s_cb, n - 1)
                for i, b in enumerate((n, k - 1)):
                    for q in range(2):
                        for j in range(2):
                            t = 2 * b + q
                            pool.indirect_dma_start(y_tok[k % 2][:, 4 * i + 2 * q + j, :], None, slots_y,
                                                    bass.IndirectOffsetOnAxis(pos[j][:, t:t + 1], 0)).then_inc(s_yg[k % 2], 16)

        @block.scalar
        def _(act):
            act.wait_ge(s_small, 64)
            act.activation(ws[:, 0, :], ws_stage, ACT.Copy, scale=WS).then_inc(s_hiw, 1)
            act.wait_ge(s_w1, 16)
            act.activation(w1[:, 0, :], w_stage[:, 0:NE * FF], ACT.Copy, scale=FS).then_inc(s_hiw, 1)
            act.wait_ge(s_w2, 16)
            act.activation(w2[:, 0, :], w_stage[:, NE * FF:2 * NE * FF], ACT.Copy, scale=FS).then_inc(s_hiw, 1)
            act.wait_ge(s_d, 1)
            act.activation(tmp[1][:, :], tmp[0][:, :], ACT.Sqrt).then_inc(s_sd, 1)
            with act.Fori(0, NT // 8, 1) as i:
                for r in range(2):
                    act.wait_ge(s_tr, 2 * i + r + 1)
                    for part in range(2):
                        act.activation(xT[:, part, bass.ds((2 * i + r) * 4 * P, 4 * P)], bank[2 * r + part][:, :], ACT.Copy).then_inc(s_xt, 1)
            act.wait_ge(s_sub, 1)
            act.activation(r_view[1], r_view[1], ACT.Exp).then_inc(s_exp8, 1)

            def attend(s, f, k):
                b, par, half = s.at(0)
                for u in range(8):
                    g = u // 2
                    if f["x"]:
                        for n in (2 * u, 2 * u + 1):
                            act.wait_ge(s_ex, 16 * b + n + 1)
                            if k != 0 or u >= 2:
                                act.wait_ge(s_pv, 8 * b + u - 1)
                            act.activation(A[:, n % 4, :, :].rearrange("p h s -> p (h s)"), EX[n % 2][:, :], ACT.Exp, scale=SCALE).then_inc(s_xp, 1)
                    if u % 2 == 0 and (f["x"] if u else f["o"]):
                        bb, pp, _ = s.at(0 if u else -1)
                        gg = g - 1 if u else 3
                        act.wait_ge(s_pv, 8 * bb + 2 * gg + 2)
                        if gg == 0 and (k is None or bb >= 2):
                            act.wait_ge(s_ot, 2 * bb - 2)
                        act.activation(O[:, pp, gg, :], PV[gg % 2][:, 0:S], ACT.Copy).then_inc(s_pe, 1)
                    if u == 0 and f["x"]:
                        act.wait_ge(s_mt, 2 * b + 2)
                        if k is None or b >= 1:
                            act.wait_ge(s_mr[1 - par][1], 16 * (s.at(-1)[2] + 1))
                        act.activation(mT[:, 1, :, :].rearrange("h q t -> h (q t)"), MISC[0][0:8, 0:S // 2].bitcast(F16), ACT.Copy).then_inc(s_mte, 1)
                    if u == 1 and f["p"]:
                        b2_, par2, half2 = s.at(2)
                        act.wait_ge(s_qk, b2_ + 1)
                        if k is None or b2_ >= 1:
                            act.wait_ge(s_wr[1 - par2], 80 * (s.at(1)[2] + 1))
                        act.activation(hi_qk[:, :, :].rearrange("p a t -> p (a t)"), MISC[1][:, :], ACT.Copy, scale=1 / WS).then_inc(s_hq, 1)
                    if u == 2 and f["p"]:
                        act.wait_ge(s_cx, b2_ + 1)
                        if f["m"]:
                            act.wait_ge(s_v, b2_)
                        act.activation(part_c[:, 0, :], MISC[0][0:DE, 0:S], ACT.Copy, scale=CTX / WS).then_inc(s_ch, 1)
                    if u == 4 and f["m"]:
                        b1_, par1, _ = s.at(1)
                        act.wait_ge(s_mt, 2 * b1_ + 1)
                        if k is None or b1_ >= 1:
                            act.wait_ge(s_mr[1 - par1][0], 16 * (s.at(0)[2] + 1))
                        act.activation(mT[:, 0, :, :].rearrange("h q t -> h (q t)"), MISC[0][0:8, 0:S // 2].bitcast(F16), ACT.Copy).then_inc(s_mte, 1)
                    if u == 6 and f["o"]:
                        bo = s.at(-1)[0]
                        act.wait_ge(s_oT, bo + 1)
                        if k is None or bo >= 1:
                            act.wait_ge(s_wo, bo)
                        act.activation(oT[:, :], MISC[0][:, 0:2 * P], ACT.Copy).then_inc(s_oTe, 1)

            attention_steps(act, 0, attend)

            def expert(quad, r, a, b, c):
                if b:
                    t = 4 * quad + r
                    e = act.value_load(tile_e[0:1, 1, bass.ds(t, 1)] if not isinstance(t, int) else tile_e[0:1, 1, t:t + 1], min_val=0, max_val=(NE - 1) * FC)
                    if not isinstance(t, int) or t >= 2:
                        act.wait_ge(s_fl, 2 * t - 2)
                    for fc in range(FC):
                        act.wait_ge(s_fu, 4 * t + fc + 1)
                        act.activation(h32[r % 2][:, fc, :], bank[fc][:, 0:SLOT], ACT.Gelu_apprx_tanh, bias=b1[:, bass.ds(e + fc, 1)], scale=1 / FS).then_inc(s_fg, 1)

            expert_steps(act, expert)
            attention_steps(act, HALF, attend)

        @block.vector
        def _(dve):
            chain = [0]

            def link(ins, n=1):
                chain[0] += n
                ins.then_inc(s_d, 1)
                dve.wait_ge(s_d, chain[0])

            def then(ins):
                chain[0] += 1
                ins.then_inc(s_d, 1)

            dve.wait_ge(s_hiw, 1)
            dve.scalar_tensor_tensor(out=ws[:, 1, :], in0=ws_stage, scalar=WS, in1=ws[:, 0, :], op0=ALU.mult, op1=ALU.subtract).then_inc(s_low, 1)
            dve.wait_ge(s_x, 16)
            with dve.Fori(0, NT // 8, 1) as i:
                for j in range(8):
                    ins = dve.bn_stats(stats[:, bass.ds(8 * i + j, 1), :].rearrange("p a s -> p (a s)"), x[:, bass.ds(8 * i + j, 1), :].rearrange("p a d -> p (a d)"))
                ins.then_inc(s_rd, 1)
            dve.wait_ge(s_rd, NT // 8)
            st = stats
            t0, t1, t2, t3 = (t[:, :] for t in tmp)
            for out_, a, b_, op in ((t1, st[:, :, 1], st[:, :, 4], ALU.add), (t2, st[:, :, 1], st[:, :, 4], ALU.subtract), (t3, st[:, :, 2], st[:, :, 5], ALU.add)):
                ins = dve.tensor_tensor(out_, a, b_, op)
            ins.then_inc(s_rd, 1)
            dve.wait_ge(s_rd, NT // 8 + 1)
            dve.tensor_scalar(mean[:, :], t1, 0.5, None, ALU.mult)
            dve.tensor_tensor(t2, t2, t2, ALU.mult)
            dve.tensor_scalar(t3, t3, 1.0 / D, EPS, ALU.mult, ALU.add).then_inc(s_rd, 1)
            dve.wait_ge(s_rd, NT // 8 + 2)
            link(dve.scalar_tensor_tensor(out=t0, in0=t2, scalar=0.25, in1=t3, op0=ALU.mult, op1=ALU.add))
            dve.wait_ge(s_sd, 1)
            link(dve.reciprocal(t2, t1))
            link(dve.tensor_tensor(t3, t2, t2, ALU.mult))
            link(dve.tensor_tensor(t3, t3, t0, ALU.mult))
            link(dve.tensor_scalar(t3, t3, -0.5, 1.5, ALU.mult, ALU.add))
            link(dve.tensor_tensor(rstd[:, :], t2, t3, ALU.mult))
            c0 = chain[0]
            with dve.Fori(0, NT // 4, 1) as i:
                for j in range(4):
                    ins = dve.tensor_scalar(xn32[:, j, :], x[:, bass.ds(4 * i + j, 1), :].rearrange("p a d -> p (a d)"),
                                            mean[:, bass.ds(4 * i + j, 1)], rstd[:, bass.ds(4 * i + j, 1)], ALU.subtract, ALU.mult)
                ins.then_inc(s_d, 1)
                dve.wait_ge(s_d, 2 * i + c0 + 1)
                hi = rows[:, bass.ds(4 * i, 4), 0:D]
                dve.tensor_copy(hi, xn32).then_inc(s_d, 1)
                dve.wait_ge(s_d, 2 * i + c0 + 2)
                dve.tensor_tensor(rows[:, bass.ds(4 * i, 4), D:2 * D], xn32, hi, ALU.subtract).then_inc(s_rows, 1)
                dve.wait_ge(s_rows, i + 1)
            chain[0] += 2 * (NT // 4)
            for n, w in enumerate((w1, w2)):
                dve.wait_ge(s_hiw, n + 2)
                dve.scalar_tensor_tensor(out=w[:, 1, :], in0=w_stage[:, n * NE * FF:(n + 1) * NE * FF], scalar=FS, in1=w[:, 0, :],
                                         op0=ALU.mult, op1=ALU.subtract).then_inc(s_low, 1)
            L, Ex, Ta, Tb = r_view
            flat = lambda v: v.rearrange("p t e -> p (t e)")
            dve.wait_ge(s_gate, NT // 4)
            link(dve.tensor_scalar(flat(L), bank[4][:, :], 1 / WS, None, ALU.mult))
            for e in range(NE):
                won = wins[:, e, :].rearrange("p (t e) -> p t e", e=NE)
                then(dve.tensor_tensor(won[:, :, 0:e + 1], L[:, :, e:e + 1].to_broadcast([P, NT, e + 1]), L[:, :, 0:e + 1], ALU.is_gt))
                if e < NE - 1:
                    then(dve.tensor_tensor(won[:, :, e + 1:NE], L[:, :, e:e + 1].to_broadcast([P, NT, NE - 1 - e]), L[:, :, e + 1:NE], ALU.is_ge))
            then(dve.tensor_reduce(tmp[0][:, :], L, AX.X, ALU.max))
            dve.wait_ge(s_d, chain[0])
            dve.tensor_tensor(Ex, L, tmp[0][:, :].unsqueeze(2).to_broadcast([P, NT, NE]), ALU.subtract).then_inc(s_sub, 1)
            link(dve.tensor_reduce(flat(Ta), wins.rearrange("p a n -> p n a"), AX.X, ALU.add))
            dve.tensor_scalar(picked[:, :], flat(Ta), 2.0, None, ALU.is_lt).then_inc(s_m, 1)
            for j in range(2):
                link(dve.tensor_scalar(flat(sel[j]), flat(Ta), float(j), None, ALU.is_equal))
            dve.wait_ge(s_exp8, 1)
            link(dve.tensor_reduce(tmp[0][:, :], Ex, AX.X, ALU.add))
            link(dve.reciprocal(tmp[1][:, :], tmp[0][:, :]))
            for j in range(2):
                link(dve.tensor_tensor(Tb, Ex, sel[j][:, :, :], ALU.mult))
                link(dve.tensor_reduce(tmp[2][:, :], Tb, AX.X, ALU.add))
                link(dve.tensor_tensor(prob[j][:, :], tmp[2][:, :], tmp[1][:, :], ALU.mult))
            dve.wait_ge(s_cnt, 1)
            link(dve.tensor_copy(flat(scan[0][:, :, :]), bank[6][:, :]))
            src, dst, d = scan[0], scan[1], 1
            link(dve.tensor_copy(flat(Ta), bank[6][:, :]))
            while d < NT:
                then(dve.tensor_copy(dst[:, 0:d, :], src[:, 0:d, :]))
                link(dve.tensor_tensor(dst[:, d:NT, :], src[:, d:NT, :], src[:, 0:NT - d, :], ALU.add))
                src, dst, d = dst, src, 2 * d
            link(dve.tensor_scalar(cnt8i[:, :], src[:, NT - 1, :], float(SLOT - 1), None, ALU.add))
            link(dve.tensor_single_scalar(cnt8i[:, :], cnt8i[:, :], SLOT.bit_length() - 1, op=ALU.logical_shift_right))
            link(dve.tensor_copy(cnt8[:, 0, :], cnt8i[:, :]))
            link(dve.tensor_copy(cnt8[:, 1, :], cnt8[:, 0, :]))
            for e in range(1, NE):
                link(dve.tensor_tensor(cnt8[:, 1, e:e + 1], cnt8[:, 1, e - 1:e], cnt8[:, 0, e:e + 1], ALU.add))
            link(dve.tensor_tensor(cnt8[:, 2, :], cnt8[:, 1, :], cnt8[:, 0, :], ALU.subtract))
            link(dve.tensor_scalar(cnt8[:, 3, :], cnt8[:, 2, :], float(SLOT), None, ALU.mult))
            link(dve.tensor_tensor(dst[:, :, :], src[:, :, :], Ta, ALU.subtract))
            link(dve.tensor_tensor(flat(Ta), bank[5][:, :], flat(dst[:, :, :]), ALU.add))
            link(dve.tensor_tensor(Ta, Ta, cnt8[:, 3, :].unsqueeze(1).to_broadcast([P, NT, NE]), ALU.add))
            for j in range(2):
                link(dve.tensor_tensor(Tb, Ta, sel[j][:, :, :], ALU.mult))
                link(dve.tensor_reduce(tmp[2][:, :], Tb, AX.X, ALU.add))
                link(dve.tensor_copy(pos[j][:, :], tmp[2][:, :]))
            tf = tile_f[:, 0:ET * NE].rearrange("p (t e) -> p t e", e=NE)
            link(dve.tensor_copy(tf, tile_no[:, :].unsqueeze(2).to_broadcast([1, ET, NE])))
            link(dve.tensor_tensor(tf, tf, cnt8[0:1, 1, :].unsqueeze(1).to_broadcast([1, ET, NE]), ALU.is_ge))
            te = tile_f[:, ET * NE:ET * NE + ET]
            link(dve.tensor_reduce(te, tf, AX.X, ALU.add))
            link(dve.tensor_scalar(te, te, float(NE - 1), None, ALU.min))
            link(dve.tensor_scalar(tile_e[:, 0, :], te, float(FF), None, ALU.mult))
            dve.tensor_scalar(tile_e[:, 1, :], te, float(FC), None, ALU.mult).then_inc(s_routed, 1)
            dve.wait_ge(s_post, NPOST)
            c_rd = NT // 8 + 2

            def attend(s, f, k):
                b, par, half = s.at(0)
                b1_, par1, half1 = s.at(1)
                for u in range(8):
                    if f["m"]:
                        g, qt = u // 2, u % 2
                        for p in range(2):
                            n = 2 * u + p
                            dve.wait_ge(s_mx, 16 * b1_ + n + 1)
                            dve.tensor_reduce(mx[:, par1, qt, 4 * g + 2 * p:4 * g + 2 * p + 2], MX[p][:, :].rearrange("q (h k) -> q h k", h=2), AX.X, ALU.max).then_inc(s_red, 1)
                        if u in (3, 7):
                            a = u // 4
                            dve.wait_ge(s_red, 16 * b1_ + 8 * a + 8)
                            if k is None or b1_ >= 1:
                                dve.wait_ge(s_mt, 2 * b1_ + a - 1)
                            dve.tensor_scalar(negm[:, a, :, :], mx[:, par1, :, 8 * a:8 * a + 8], -1.0, None, ALU.mult).then_inc(s_nm, 1)
                    if u == 1 and f["p"]:
                        b2_ = s.at(2)[0]
                        dve.wait_ge(s_hq, b2_ + 1)
                        dve.scalar_tensor_tensor(out=lo_qk[:, :, :].rearrange("p a t -> p (a t)"), in0=MISC[1][:, :], scalar=1 / WS,
                                                 in1=hi_qk[:, :, :].rearrange("p a t -> p (a t)"), op0=ALU.mult, op1=ALU.subtract).then_inc(s_lq, 1)
                    if u == 2 and f["p"]:
                        dve.wait_ge(s_ch, b2_ + 1)
                        dve.scalar_tensor_tensor(out=part_c[:, 1, :], in0=MISC[0][0:DE, 0:S], scalar=CTX / WS, in1=part_c[:, 0, :],
                                                 op0=ALU.mult, op1=ALU.subtract).then_inc(s_cl, 1)
                    if u == 2 and f["m"]:
                        dve.wait_ge(s_v, b1_ + 1)
                        if k is None or b1_ >= 2:
                            dve.wait_ge(s_pv, 8 * b1_ - 8)
                        dve.tensor_scalar(V[:, par1, :, :, 0:DK], MISC[0][:, S:2 * S].rearrange("p (c h d) -> p c h d", c=2, d=DK), 1 / WS, None, ALU.mult).then_inc(s_vc, 1)
                    if u in (3, 5) and f["o"]:
                        bo = s.at(-1)[0]
                        qt = (u - 3) // 2
                        dve.wait_ge(s_ot, 2 * bo + qt + 1)
                        v = MISC[1][:, :].rearrange("q (h r) -> q h r", r=32)
                        dve.reciprocal(rden[:, qt, :], v[:, :, DK]).then_inc(s_rd, 1)
                        dve.wait_ge(s_rd, 2 * bo + qt + 1 + c_rd)
                        if qt == 0 and (k is None or bo >= 1):
                            dve.wait_ge(s_oT, bo)
                        dve.tensor_tensor(o_n[:, qt, :, :], v[:, :, 0:DK], rden[:, qt, :].unsqueeze(2).to_broadcast([P, H, DK]), ALU.mult).then_inc(s_on, 1)
                    if u == 7 and f["o"]:
                        dve.wait_ge(s_wo, bo + 1)
                        xs_ = x[:, 2 * bo:2 * bo + 2, :] if isinstance(bo, int) else x[:, bass.ds(2 * bo, 2), :]
                        dve.tensor_tensor(xs_, xs_, MISC[1][:, 0:2 * P].rearrange("p (q d) -> p q d", q=2), ALU.add).then_inc(s_acc, 1)

            attention_steps(dve, 0, attend)

            def expert(quad, r, a, b, c):
                t = 4 * quad + r
                static = isinstance(t, int)
                if a:
                    n, par = t + 1, (r + 1) % 2
                    dve.wait_ge(s_ft, n + 1)
                    if not static or n >= 2:
                        dve.wait_ge(s_fu, 4 * n - 4)
                    dve.tensor_copy(xt[par].rearrange("p a s -> p (a s)"), bank[4 + par][:, 0:SLOT].bitcast(F16)).then_inc(s_fx, 1)
                if b:
                    par = r % 2
                    for hf in range(2):
                        dve.wait_ge(s_fg, 4 * t + 2 * hf + 2)
                        if hf == 0 and (not static or t >= 2):
                            dve.wait_ge(s_fd, t - 1)
                        hi, lo, h = (v[:, 2 * hf:2 * hf + 2, :] for v in (hp[par][:, 0], hp[par][:, 1], h32[par]))
                        dve.tensor_copy(hi, h).then_inc(s_fh, 1)
                        dve.wait_ge(s_fh, 2 * t + hf + 1)
                        dve.tensor_tensor(lo, h, hi, ALU.subtract).then_inc(s_fl, 1)
                if c:
                    n, par = t - 1, (r - 1) % 2
                    e = dve.value_load(tile_e[0:1, 1, n:n + 1] if static else tile_e[0:1, 1, bass.ds(n, 1)], min_val=0, max_val=(NE - 1) * FC)
                    dve.wait_ge(s_fd, n + 1)
                    if not static or n >= 2:
                        dve.wait_ge(s_ys[par], 16 * (2 * quad + (r - 1) // 2))
                    dve.scalar_tensor_tensor(out=ye[par], in0=bank[6 + par][:, 0:2 * D].rearrange("p (s d) -> p s d", s=2), scalar=1 / FS,
                                             in1=b2[:, bass.ds(e * (D // FC), D)].unsqueeze(1).to_broadcast([P, 2, D]), op0=ALU.mult, op1=ALU.add).then_inc(s_fy, 1)

            expert_steps(dve, expert)

            def attend_combine(s, f, k):
                attend(s, f, k)
                if f["o"]:
                    bo, po, _ = s.at(-1)
                    par = 1 - po
                    dve.wait_ge(s_yg[par], 128 * (s.half - (HALF // 2) + (1 if s.r else 0)))
                    dve.wait_ge(s_acc, bo + 1)
                    for j in range(2):
                        for i, bb in enumerate((bo - HALF, bo)):
                            for q in range(2):
                                t = 2 * bb + q
                                if isinstance(t, int):
                                    xx, pr = x[:, t, :], prob[j][:, t:t + 1]
                                else:
                                    xx, pr = x[:, bass.ds(t, 1), :].rearrange("p a d -> p (a d)"), prob[j][:, bass.ds(t, 1)]
                                ins = dve.scalar_tensor_tensor(out=xx, in0=y_tok[par][:, 4 * i + 2 * q + j, :], scalar=pr, in1=xx, op0=ALU.mult, op1=ALU.add)
                        ins.then_inc((s_c1, s_cb)[j], 1)
                        if j == 0:
                            dve.wait_ge(s_c1, bo - HALF + 1)

            attention_steps(dve, HALF, attend_combine)

        @block.tensor
        def _(pe):
            pe.wait_ge(s_const, NCONST)
            pe.wait_ge(s_low, 1)

            with pe.Fori(0, NT // 8, 1) as i:
                for r in range(2):
                    pe.wait_ge(s_rows, 2 * i + r + 1)
                    for part in range(2):
                        for j in range(4):
                            t = 8 * i + 4 * r + j
                            mm = pe.matmul(bank[2 * r + part][:, j * P:(j + 1) * P], rows[:, bass.ds(t, 1), part * D:(part + 1) * D].rearrange("p a d -> p (a d)"),
                                           ident16[:, :], start=True, stop=True)
                    mm.then_inc(s_tr, 1)
                for r in range(2):
                    pe.wait_ge(s_xt, 4 * i + 2 * r + 2)
                    for j in range(4):
                        t = 8 * i + 4 * r + j
                        for n, (pa, pb) in enumerate(TERMS):
                            mm = pe.matmul(bank[4][:, bass.ds(t * NE, NE)], xT[:, pa, bass.ds(t * P, P)], ws[:, pb, CG:CG + NE], start=(n == 0), stop=(n == 2))
                    mm.then_inc(s_gate, 1)
            pe.wait_ge(s_m, 1)
            pe.matmul(bank[5][:, :], before[:, :], picked[:, :], start=True, stop=True)
            pe.matmul(bank[6][:, :], ones16[:, :], picked[:, :], start=True, stop=True).then_inc(s_cnt, 1)
            pe.wait_ge(s_routed, 1)

            def drained(e, s, f, k):
                def readers(e, off, f, k):
                    n = lambda o: s.at(off + o)[0]
                    return {0: f["x"] and [(s_mte, 2 * n(0) + 2)], 1: f["p"] and [(s_lq, n(2) + 1)],
                            2: (f["p"] or f["m"]) and [(s_cl, n(2) + 1)] * f["p"] + [(s_vc, n(1) + 1)] * f["m"],
                            3: f["o"] and [(s_on, 2 * n(-1) + 1)], 4: f["m"] and [(s_mte, 2 * n(1) + 1)],
                            5: f["o"] and [(s_on, 2 * n(-1) + 2)], 6: f["o"] and [(s_oTe, n(-1) + 1)],
                            7: f["o"] and [(s_acc, n(-1) + 1)]}[e]
                off, ee = 0, e - 2
                while True:
                    if ee < 0:
                        ee += 8
                        off -= 1
                        if k is not None:
                            if off < -2:
                                return
                            f = attention_flags(k + off, HALF * (0 if k < HALF + 1 and phase[0] == 0 else 1))
                    got = readers(ee, off, f, k)
                    if got:
                        for sm, v in got:
                            if not isinstance(v, int) or v > 0:
                                pe.wait_ge(sm, v)
                        return
                    ee -= 2

            phase = [0]

            def xcols(part, b, n=S, o=0):
                return xT[:, part, b * S + o:b * S + o + n] if isinstance(b, int) else xT[:, part, bass.ds(b * S + o, n)]

            def attend(s, f, k):
                b, par, half = s.at(0)
                b1_, par1, half1 = s.at(1)
                b2_ = s.at(2)[0]
                bo, paro, _ = s.at(-1)

                def values(bb, pp, v):
                    g, c = v // 2, v % 2
                    pe.wait_ge(s_xp, 16 * bb + 2 * v + 2)
                    if v == 0:
                        pe.wait_ge(s_vc, bb + 1)
                    if c == 0 and (not isinstance(bb, int) or 4 * bb + g >= 2):
                        pe.wait_ge(s_pe, 4 * bb + g - 1)
                    for i in range(4):
                        mm = pe.matmul(PV[g % 2][32 * i:32 * i + 32, 0:S], V[:, pp, c, 4 * g + i, :], A[:, (2 * v + i // 2) % 4, i % 2, :],
                                       start=(c == 0), stop=(c == 1))
                    mm.then_inc(s_pv, 1)

                for u in range(8):
                    g, c = u // 2, u % 2
                    if f["x"]:
                        if u in (0, 4):
                            pe.wait_ge(s_mr[par][u // 4], 16 * (half + 1))
                        for p in range(2):
                            n = 2 * u + p
                            if not isinstance(b, int) or 16 * b + n >= 2:
                                pe.wait_ge(s_xp, 16 * b + n - 1)
                            for i in range(2):
                                h = 4 * g + 2 * p + i
                                mm = pe.matmul(EX[p][:, i * S:(i + 1) * S], stack[0:ROWS + 1, par, 1, h, c * P:(c + 1) * P], stack[0:ROWS + 1, par, 0, h, :], start=True, stop=True)
                            mm.then_inc(s_ex, 1)
                    if f["m"]:
                        if c == 0:
                            pe.wait_ge(s_st[par1][g], 128 * (half1 + 1))
                        for p in range(2):
                            n = 2 * u + p
                            if not isinstance(b1_, int) or 16 * b1_ + n >= 2:
                                pe.wait_ge(s_red, 16 * b1_ + n - 1)
                            for i in range(2):
                                h = 4 * g + 2 * p + i
                                mm = pe.matmul(MX[p][:, i * S:(i + 1) * S], stack[0:ROWS, par1, 0, h, c * P:(c + 1) * P], stack[0:ROWS, par1, 1, h, :], start=True, stop=True)
                            mm.then_inc(s_mx, 1)
                    if u == 0 and f["o"]:
                        values(bo, paro, 7)
                    if u > 0 and f["x"]:
                        values(b, par, u - 1)
                    M = MISC[u % 2]
                    if (u == 0 and f["x"]) or (u == 4 and f["m"]):
                        a = 1 if u == 0 else 0
                        drained(u, s, f, k)
                        pe.wait_ge(s_nm, 2 * (b if u == 0 else b1_) + a + 1)
                        for q in range(2):
                            mm = pe.transpose(M[0:8, 0:S // 2].bitcast(F16)[:, q * P:(q + 1) * P], negm[:, a, q, :], ident16[:, :])
                        mm.then_inc(s_mt, 1)
                    if u == 1 and f["p"]:
                        drained(u, s, f, k)
                        for side, col in ((0, CQ), (1, CK)):
                            for n, (pa, pb) in enumerate(TERMS):
                                mm = pe.matmul(M[:, side * S:(side + 1) * S], ws[:, pa, col:col + D], xcols(pb, b2_), start=(n == 0), stop=(n == 2))
                        mm.then_inc(s_qk, 1)
                    if u == 2 and (f["p"] or f["m"]):
                        drained(u, s, f, k)
                        if f["m"]:
                            for q in range(2):
                                for n, (pa, pb) in enumerate(TERMS):
                                    mm = pe.matmul(M[:, S + q * P:S + (q + 1) * P], xcols(pa, b1_, P, q * P), ws[:, pb, CV:CV + D], start=(n == 0), stop=(n == 2))
                            mm.then_inc(s_v, 1)
                        if f["p"]:
                            for n, (pa, pb) in enumerate(TERMS):
                                mm = pe.matmul(M[0:DE, 0:S], ws[:, pa, CE:CE + DE], xcols(pb, b2_), start=(n == 0), stop=(n == 2))
                            mm.then_inc(s_cx, 1)
                    if u in (3, 5) and f["o"]:
                        drained(u, s, f, k)
                        qt = (u - 3) // 2
                        if qt == 0:
                            pe.wait_ge(s_pe, 4 * bo + 4)
                        for gg in range(4):
                            mm = pe.transpose(M[:, gg * P:(gg + 1) * P], O[:, paro, gg, qt * P:(qt + 1) * P], ident[:, :])
                        mm.then_inc(s_ot, 1)
                    if u == 6 and f["o"]:
                        drained(u, s, f, k)
                        pe.wait_ge(s_on, 2 * bo + 2)
                        for q in range(2):
                            mm = pe.transpose(M[:, q * P:(q + 1) * P], o_n[:, q, :, :].rearrange("p h d -> p (h d)"), ident[:, :])
                        mm.then_inc(s_oT, 1)
                    if u == 7 and f["o"]:
                        drained(u, s, f, k)
                        pe.wait_ge(s_oTe, bo + 1)
                        for q in range(2):
                            mm = pe.matmul(M[:, q * P:(q + 1) * P], oT[:, q * P:(q + 1) * P], wo[:, :], start=True, stop=True)
                        mm.then_inc(s_wo, 1)

            attention_steps(pe, 0, attend)
            for sm, n in ((s_acc, HALF), (s_red, 16 * HALF), (s_xp, 16 * HALF), (s_pe, 4 * HALF), (s_vc, HALF), (s_oTe, HALF)):
                pe.wait_ge(sm, n)

            def expert(quad, r, a, b, c):
                t = 4 * quad + r
                static = isinstance(t, int)

                def first_col(n):
                    return pe.value_load(tile_e[0:1, 0, n:n + 1] if static else tile_e[0:1, 0, bass.ds(n, 1)], min_val=0, max_val=(NE - 1) * FF)

                if a:
                    n, par, r4 = t + 1, (r + 1) % 2, (r + 1) % 4
                    pe.wait_ge(s_xr[r4], 16 * (quad + (r + 1) // 4 + 1))
                    if not static or n >= 2:
                        pe.wait_ge(s_fx, n - 1)
                    v = bank[4 + par][:, 0:SLOT].bitcast(F16)
                    for part in range(2):
                        for h in range(2):
                            mm = pe.transpose(v[:, part * SLOT + h * P:part * SLOT + (h + 1) * P], xr[r4][:, h, part * D:(part + 1) * D], ident16[:, :])
                    mm.then_inc(s_ft, 1)
                if b:
                    e = first_col(t)
                    pe.wait_ge(s_fx, t + 1)
                    for fc in range(FC):
                        if not static or t >= 1:
                            pe.wait_ge(s_fg, 4 * t + fc - 3)
                        for n, (pa, pb) in enumerate(TERMS):
                            mm = pe.matmul(bank[fc][:, 0:SLOT], w1[:, pa, bass.ds(e + fc * P, P)], xt[r % 2][:, pb, :], start=(n == 0), stop=(n == 2))
                        mm.then_inc(s_fu, 1)
                if c:
                    n, par = t - 1, (r - 1) % 2
                    e = first_col(n)
                    pe.wait_ge(s_fl, 2 * n + 2)
                    if not static or n >= 2:
                        pe.wait_ge(s_fy, n - 1)
                    for h in range(2):
                        for fc in range(FC):
                            for m, (pa, pb) in enumerate(TERMS):
                                mm = pe.matmul(bank[6 + par][:, h * D:(h + 1) * D], hp[par][:, pa, fc, h * P:(h + 1) * P], w2[:, pb, bass.ds(e + fc * P, P)],
                                               start=(fc == 0 and m == 0), stop=(fc == FC - 1 and m == 2))
                    mm.then_inc(s_fd, 1)

            expert_steps(pe, expert)
            for sm, n in ((s_fy, ET), (s_fg, FC * ET), (s_fx, ET)):
                pe.wait_ge(sm, n)
            phase[0] = 1
            attention_steps(pe, HALF, attend)


def kernel(L0_attn_X, L0_attn_Wq, L0_attn_Wk, L0_attn_Wv, L0_attn_Wo, L0_attn_We, L0_ffn_gate_w, L0_ffn_w1, L0_ffn_b1, L0_ffn_w2, L0_ffn_b2):
    import numpy as np
    import concourse.bacc as bacc
    from concourse.bass_utils import run_bass_kernel_spmd

    turned = [np.asarray(w).T for w in (L0_attn_Wq, L0_attn_Wk, L0_attn_Wv, L0_attn_We, L0_ffn_gate_w)]
    w2 = np.asarray(L0_ffn_w2).transpose(1, 2, 0).reshape(NE, FC, P, D).transpose(2, 0, 1, 3)
    arrays = {
        "x": np.asarray(L0_attn_X).reshape(B * S, D),
        "wsmall": np.concatenate(turned, axis=1),
        "wo": np.asarray(L0_attn_Wo).T,
        "w1": np.asarray(L0_ffn_w1).transpose(2, 1, 0).reshape(D, NE * FF),
        "w2": w2.reshape(P, NE * FF),
        "b1": np.asarray(L0_ffn_b1).reshape(NE * FC, P).T,
        "b2": np.asarray(L0_ffn_b2).reshape(1, NE * D),
    }
    arrays = {f"in_{n}": np.ascontiguousarray(a) for n, a in arrays.items()}
    nc = bacc.Bacc("TRN2", target_bir_lowering=False, num_devices=1)
    ins = [nc.dram_tensor(n, list(a.shape), mybir.dt.from_np(a.dtype), kind="ExternalInput").ap() for n, a in arrays.items()]
    out = nc.dram_tensor("out_rows", [B * S, D], F32, kind="ExternalOutput").ap()
    build(nc, *ins, out)
    r = run_bass_kernel_spmd(nc, [arrays], core_ids=[0])
    return np.asarray(r.results[0]["out_rows"]).reshape(B, S, D)
```

```python
from contextlib import ExitStack

import concourse.bass as bass
from concourse import mybir

F32 = mybir.dt.float32
F16 = mybir.dt.float16
I32 = mybir.dt.int32
U32 = mybir.dt.uint32
ALU = mybir.AluOpType
ACT = mybir.ActivationFunctionType
AX = mybir.AxisListType

P = 128
D = 128
B = 32
S = 256
H = 16
DK = D // H
DE = D // 8
NE = 8
FF = 512
FC = FF // P
NT = B * S // P
EPS = 1e-5
SLOT = 256
ET = -(-(2 * B * S) // SLOT) + NE
UNROLL = 8
DIGIT = 3
ROWS = 3 * DK + 3 * DE
WCH = 1024
WS = 2.0 ** 8
FS = 2.0 ** 10
SCALE = DK ** -0.5
CTX = (0.1 / SCALE) ** 0.5
HALF = B // 2
NW = 3 * D + DE + NE
CQ, CK, CV, CE, CG = 0, D, 2 * D, 3 * D, 3 * D + DE
TERMS = ((0, 0), (0, 1), (1, 0))


class Step:

    def __init__(self, half, r):
        self.half, self.r = half, r

    def at(self, off):
        n = self.r + off
        return 2 * self.half + n, n % 2, self.half + n // 2


def attention_flags(k, b0):
    first, last = (0, HALF - 1) if b0 == 0 else (b0, B - 1)
    ahead = {"p": 2, "m": 1}
    return {s: first + (ahead.get(s, 0) if b0 else 0) <= k + off <= last + (0 if b0 else ahead.get(s, 0))
            for s, off in (("p", 2), ("m", 1), ("x", 0), ("o", -1), ("c", -2))}


ALL = dict.fromkeys("pmxoc", True)


def attention_steps(eng, b0, body):
    for k in range(b0 if b0 else -2, b0 + 2):
        body(Step(k // 2, k % 2), attention_flags(k, b0), k)
    with eng.Fori(b0 // 2 + 1, b0 // 2 + HALF // 2 - 1, 1) as half:
        for r in range(2):
            body(Step(half, r), ALL, None)
    for k in range(b0 + HALF - 2, b0 + HALF + 2):
        body(Step(k // 2, k % 2), attention_flags(k, b0), k)


def lagged(eng, n, body):
    body(0, True, False)
    with eng.Fori(1, n, 1) as i:
        body(i, True, True)
    body(n, False, True)


def expert_steps(eng, body, load=None):
    last = 5 + UNROLL * ((ET - 7) // UNROLL)
    load = load or (lambda n, count: [None] * count)
    e = load(0, 5)
    for t in range(-1, 5):
        body(t // 4, t % 4, t + 1 < ET, t >= 0, t >= 1, e[max(t, 0)], e[max(t - 1, 0)])
    with eng.Fori(0, (last - 5) // UNROLL, 1) as i:
        quad = UNROLL // 4 * i + 1
        e = load(quad, UNROLL + 1)
        for r in range(1, UNROLL + 1):
            body(quad, r, True, True, True, e[r], e[r - 1])
    e = load((last - 1) // 4, ET - last + 1)
    for t in range(last, ET + 1):
        body(t // 4, t % 4, t + 1 < ET, t < ET, True, e[min(t, ET - 1) - last + 1], e[t - last])


def expert_numbers(nc, eng, words, unit):
    def load(quad, count):
        nw = max((count - 1) // 4, 1)
        word = nc.values_load_multi_w_load_instructions(words[:, bass.ds(quad, nw)], engines=[eng.engine], min_val=0, max_val=(NE ** 5 - 1) * unit)[1]
        digits = [(min(j // 4, nw - 1), j) for j in range(count)]
        return [eng.snap((word[w] >> (DIGIT * (j - 4 * w))) & ((NE - 1) * unit)) for w, j in digits]
    return load


def build(nc, X, Wsmall, Wo, W12, B1, B2, out):
    with ExitStack() as ctx:
        def sb(name, shape, dt):
            return ctx.enter_context(nc.sbuf_tensor(name, shape, dt))

        def sem(name):
            return ctx.enter_context(nc.semaphore(name))

        slots_x = nc.dram_tensor("slots_x", [ET * SLOT, 2 * D], F16, kind="Internal").ap()
        slots_y = nc.dram_tensor("slots_y", [ET * SLOT, D], F32, kind="Internal").ap()
        qk_dram = nc.dram_tensor("qk_dram", [2, 2, 3 * DK, H * S], F16, kind="Internal").ap()
        ctx_dram = nc.dram_tensor("ctx_dram", [2, 5 * DE, S], F16, kind="Internal").ap()

        x = sb("x", [P, NT, D], F32)
        rows = sb("rows", [P, NT, 2 * D], F16)
        xT = sb("xT", [P, 2, B * S], F16)
        w12 = sb("w12", [P, 2, 2 * NE * FF], F16)
        w_stage = sb("w_stage", [P, WCH], F32)
        w1, w2 = w12[:, :, 0:NE * FF], w12[:, :, NE * FF:2 * NE * FF]
        ws = sb("ws", [P, 2, NW], F16)
        wo = sb("wo", [P, D], F32)
        b1 = sb("b1", [P, NE * FC], F32)
        stack = sb("stack", [P, 2, 2, H, S], F16)
        A = sb("A", [P, 4, 2, S], F32)
        V = sb("V", [P, 2, 2, H, 32], F32)
        O = sb("O", [P, 2, 4, S], F32)
        hi_qk = sb("hi_qk", [P, 2, S], F16)
        lo_qk = sb("lo_qk", [P, 2, S], F16)
        part_c = sb("part_c", [DE, 2, S], F16)
        mx = sb("mx", [P, 2, 2, H], F32)
        negm = sb("negm", [P, 2, 2, 8], F16)
        mT = sb("mT", [8, 2, 2, P], F16)
        rden = sb("rden", [P, 2, H], F32)
        o_n = sb("o_n", [P, 2, H, DK], F32)
        oT = sb("oT", [P, 2 * P], F32)
        ident = sb("ident", [P, P], F32)
        ident16 = sb("ident16", [P, P], F16)
        before = sb("before", [P, P], F16)
        ones16 = sb("ones16", [P, P], F16)
        zeros = sb("zeros", [P, 2 * D], F16)
        stats = sb("stats", [P, NT, 6], F32)
        mean = sb("mean", [P, NT], F32)
        rstd = sb("rstd", [P, NT], F32)
        shift = sb("shift", [P, NT], F32)
        tmp = [sb(f"tmp{i}", [P, NT], F32) for i in range(4)]
        prob = [sb(f"prob{i}", [P, NT], F32) for i in range(2)]
        pos = [sb(f"pos{i}", [P, NT], U32) for i in range(2)]
        picked = sb("picked", [P, NT * NE], F16)
        cnt8 = sb("cnt8", [P, 4, NE], F32)
        cnt8i = sb("cnt8i", [P, NE], I32)
        tile_no = sb("tile_no", [1, ET + 4], I32)
        tile_e = sb("tile_e", [1, 2, ET // 4], I32)

        early = w12[:, :, :].rearrange("p a n -> p (a n)")
        taken = [0]

        def temp(n):
            taken[0] += 2 * n
            return early[:, taken[0] - 2 * n:taken[0]].bitcast(F32)

        xn32 = [temp(4 * D).rearrange("p (j d) -> p j d", d=D) for _ in range(2)]
        ws_stage = temp(NW)
        L, Ex, Ta, Tb, scan0, scan1, sel0, sel1, before_tok = (temp(NT * NE).rearrange("p (t e) -> p t e", e=NE) for _ in range(9))
        scan, sel = (scan0, scan1), (sel0, sel1)
        wins32 = temp(NE * NT * NE // 2)
        wins = wins32.bitcast(F16).rearrange("p (a n) -> p a n", a=NE)
        tile_f = wins32[0:1, 0:(ET + 4) * (NE + 1) + ET // 4]
        assert taken[0] <= 4 * NE * FF
        free = rows[:, :, :].rearrange("p t d -> p (t d)")
        at = [0]

        def carve(n, dt):
            v = free[:, at[0]:at[0] + n * (2 if dt == F32 else 1)]
            at[0] += n * (2 if dt == F32 else 1)
            return v.bitcast(F32) if dt == F32 else v

        xr = [carve(2 * 2 * D, F16).rearrange("p (s c) -> p s c", s=2) for _ in range(4)]
        xt = [carve(2 * SLOT, F16).rearrange("p (a s) -> p a s", a=2) for _ in range(2)]
        h32 = [carve(FC * SLOT, F32).rearrange("p (f s) -> p f s", f=FC) for _ in range(2)]
        hp = [carve(2 * FC * SLOT, F16).rearrange("p (a f s) -> p a f s", a=2, f=FC) for _ in range(2)]
        ye = [carve(2 * D, F32).rearrange("p (s d) -> p s d", s=2) for _ in range(2)]
        b2 = carve(NE * D, F32)
        assert at[0] <= NT * 2 * D
        at[0] = 0
        y_tok = [carve(8 * D, F32).rearrange("p (j d) -> p j d", j=8) for _ in range(2)]

        bank = [ctx.enter_context(nc.psum_tensor(f"bank{i}", [P, 512], F32)) for i in range(8)]
        MX, EX, PV, MISC = bank[0:2], bank[2:4], bank[4:6], bank[6:8]

        s_x = [sem(f"s_x{q}") for q in range(4)]
        s_ws, s_small, s_wst, s_b2 = sem("s_ws"), sem("s_small"), sem("s_wst"), sem("s_b2")
        s_xa, s_xb, s_whi, s_wlo, s_cntr = (sem(n) for n in ("s_xa", "s_xb", "s_whi", "s_wlo", "s_cntr"))
        s_const, s_zero, s_post = sem("s_const"), sem("s_zero"), sem("s_post")
        s_hiw, s_low = sem("s_hiw"), sem("s_low")
        s_d, s_sd, s_rows, s_tr, s_xt, s_gate = (sem(n) for n in ("s_d", "s_sd", "s_rows", "s_tr", "s_xt", "s_gate"))
        s_sub, s_exp8, s_m, s_cnt, s_routed, s_scat = (sem(n) for n in ("s_sub", "s_exp8", "s_m", "s_cnt", "s_routed", "s_scat"))
        s_qk, s_hq, s_lq, s_cx, s_ch, s_cl, s_v, s_vc = (sem(n) for n in ("s_qk", "s_hq", "s_lq", "s_cx", "s_ch", "s_cl", "s_v", "s_vc"))
        s_wr = [sem(f"s_wr{i}") for i in range(2)]
        s_st = [[sem(f"s_st{i}_{g}") for g in range(2)] for i in range(2)]
        s_mr = [[sem(f"s_mr{i}_{a}") for a in range(2)] for i in range(2)]
        s_mx, s_red, s_nm, s_mt, s_mte = (sem(n) for n in ("s_mx", "s_red", "s_nm", "s_mt", "s_mte"))
        s_ex, s_xp, s_pv, s_pe = (sem(n) for n in ("s_ex", "s_xp", "s_pv", "s_pe"))
        s_ot, s_rd, s_on, s_oT, s_oTe, s_wo, s_acc = (sem(n) for n in ("s_ot", "s_rd", "s_on", "s_oT", "s_oTe", "s_wo", "s_acc"))
        s_xr = [sem(f"s_xr{i}") for i in range(4)]
        s_ft, s_fx, s_fu, s_fg, s_fh, s_fl, s_fd, s_fy = (sem(n) for n in ("s_ft", "s_fx", "s_fu", "s_fg", "s_fh", "s_fl", "s_fd", "s_fy"))
        s_ys = [sem(f"s_ys{i}") for i in range(2)]
        s_yg = [sem(f"s_yg{i}") for i in range(2)]
        s_c1, s_cb, s_out = sem("s_c1"), sem("s_cb"), sem("s_out")

        block = ctx.enter_context(nc.Block())
        NCONST, NPOST = 10, 4
        NCH = 2 * NE * FF // WCH

        def chunk_of(s, k, first_half):
            if not first_half or (k is not None and k not in (HALF - 2, HALF - 1)):
                return None
            if s.r == 0:
                return s.half - 1
            return NCH - 1 if k == HALF - 1 else None


        def stage_off(s, off):
            n = s.r + off
            return n % 2

        @block.sync
        def _(sp):
            sp.dma_start(ws_stage, Wsmall).then_inc(s_ws, 16)
            for q, sm in enumerate(s_x):
                n = slice(q * NT // 4, (q + 1) * NT // 4)
                sp.dma_start(x[:, n, :], X.rearrange("(t p) d -> p t d", p=P)[:, n, :]).then_inc(sm, 16)
            sp.dma_start(wo[:, :], Wo).then_inc(s_small, 16)
            sp.dma_start(b1[:, :], B1).then_inc(s_small, 16)
            sp.dma_start(w_stage[:, :], W12[:, 0:WCH]).then_inc(s_wst, 16)
            sp.wait_ge(s_const, NCONST)
            zero_rows = slots_x.rearrange("(n p) c -> p n c", p=P)
            sp.dma_start(zero_rows, zeros[:, :].unsqueeze(1).to_broadcast([P, ET * SLOT // P, 2 * D])).then_inc(s_zero, 16)
            sp.wait_ge(s_post, NPOST)

            def attend(s, f, k, first_half=True):
                b, par, half = s.at(0)
                if f["p"]:
                    b2_, par2, half2 = s.at(2)
                    sp.wait_ge(s_lq, b2_ + 1)
                    if k is None or b2_ >= 2:
                        for g in range(2):
                            sp.wait_ge(s_st[par2][g], 64 * half2)
                    for side, parts in enumerate(((hi_qk, lo_qk, hi_qk), (hi_qk, hi_qk, lo_qk))):
                        for n, src in enumerate(parts):
                            dst = qk_dram[par2, side, n * DK:(n + 1) * DK, :].rearrange("d (h t) -> h d t", t=S)
                            sp.dma_start(dst, src[:, side, :]).then_inc(s_wr[par2], 16)
                    sp.wait_ge(s_cl, b2_ + 1)
                    for lo, hi in ((0, 2), (2, 3), (3, 5)):
                        sp.dma_start(ctx_dram[par2, lo * DE:hi * DE, :].rearrange("(a c) t -> c a t", c=DE), part_c[:, 0:hi - lo, :]).then_inc(s_wr[par2], 16)
                    sp.wait_ge(s_wr[par2], 144 * (half2 + 1))
                    for g in range(2):
                        if k is None or k >= 0:
                            sp.wait_ge(s_ex, 16 * b + 8 * g + 8)
                        for side in range(2):
                            st = stack[:, par2, side, 8 * g:8 * g + 8, :]
                            sp.dma_start(st[0:3 * DK], qk_dram[par2, side, :, 8 * g * S:(8 * g + 8) * S].rearrange("r (h t) -> r h t", t=S)).then_inc(s_st[par2][g], 16)
                            c = ctx_dram[par2, 2 * side * DE:(2 * side + 3) * DE]
                            sp.dma_start(st[3 * DK:ROWS], c.unsqueeze(1).to_broadcast([3 * DE, 8, S])).then_inc(s_st[par2][g], 16)
                c = chunk_of(s, k, first_half)
                if c is not None and not (isinstance(c, int) and c == NCH - 1):
                    sp.wait_ge(s_wlo, c + 1)
                    src = W12[:, (c + 1) * WCH:(c + 2) * WCH] if isinstance(c, int) else W12[:, bass.ds((c + 1) * WCH, WCH)]
                    sp.dma_start(w_stage[:, :], src).then_inc(s_wst, 16)

            attention_steps(sp, 0, attend)

            xs = slots_x.rearrange("(n s p) c -> n p s c", s=2, p=P)
            ys = slots_y.rearrange("(n s p) d -> n p s d", s=2, p=P)
            sp.wait_ge(s_scat, 16 * 2 * NT)
            sp.dma_start(b2, B2.to_broadcast([P, NE * D])).then_inc(s_b2, 16)

            def expert(quad, r, a, b, c, e, e_before):
                t = 4 * quad + r
                if a:
                    todo = [(quad + (r + 3) // 4, (r + 3) % 4)]
                    if isinstance(quad, int):
                        todo = [(n // 4, n % 4) for n in ((0, 1, 2) if t < 0 else (t + 3,)) if n < ET]
                    for q2, r2 in todo:
                        n = 4 * q2 + r2
                        if not isinstance(n, int) or n >= 4:
                            sp.wait_ge(s_ft, n - 3)
                        if isinstance(n, int):
                            src = xs[n]
                        else:
                            src = xs[bass.ds(n, 1)].rearrange("n p s c -> (n p) s c")
                        sp.dma_start(xr[r2], src).then_inc(s_xr[r2], 16)
                if c:
                    n = t - 1
                    sp.wait_ge(s_fy, n + 1)
                    dst = ys[n] if isinstance(n, int) else ys[bass.ds(n, 1)].rearrange("n p s d -> (n p) s d")
                    sp.dma_start(dst, ye[(r - 1) % 2]).then_inc(s_ys[(r - 1) % 2], 16)

            expert_steps(sp, expert)

            out_v = out.rearrange("(n s p) d -> n p s d", s=2, p=P)

            def attend_store(s, f, k):
                attend(s, f, k, False)
                if f["c"]:
                    b = s.at(-2)[0]
                    sp.wait_ge(s_cb, b - HALF + 1)
                    for n in (b - HALF, b):
                        if isinstance(n, int):
                            sp.dma_start(out_v[n], x[:, 2 * n:2 * n + 2, :]).then_inc(s_out, 16)
                        else:
                            sp.dma_start(out_v[bass.ds(n, 1)].rearrange("n p s d -> (n p) s d"), x[:, bass.ds(2 * n, 2), :]).then_inc(s_out, 16)

            attention_steps(sp, HALF, attend_store)
            sp.wait_ge(s_out, 16 * B)

        @block.gpsimd
        def _(pool):
            c = [0]

            def const(ins, wait=False):
                c[0] += 1
                ins.then_inc(s_const, 1)
                if wait:
                    pool.wait_ge(s_const, c[0])

            const(pool.memset(zeros[:, :], 0.0))
            const(pool.memset(ident[:, :], 0.0))
            const(pool.memset(ident16[:, :], 0.0))
            const(pool.memset(before[:, :], 1.0))
            const(pool.memset(ones16[:, :], 1.0), wait=True)
            for m in (ident, ident16):
                const(pool.affine_select(out=m[:, :], in_=m[:, :], compare_op=ALU.not_equal, fill=1.0, base=0,
                                         pattern=[[-1, P]], channel_multiplier=1))
            const(pool.affine_select(out=before[:, :], in_=before[:, :], compare_op=ALU.is_gt, fill=0.0, base=0,
                                     pattern=[[1, P]], channel_multiplier=-1))
            const(pool.iota(tile_no[:, :], pattern=[[1, ET + 4]], base=0, channel_multiplier=0))
            const(pool.memset(cnt8[:, 3, :], 0.0), wait=True)
            assert c[0] == NCONST
            for par in range(2):
                pool.memset(stack[64:ROWS + 1, par, 1, :, :], 1.0).then_inc(s_post, 1)
                pool.wait_ge(s_post, par + 1)
            pool.memset(V[:, :, :, :, :], 0.0).then_inc(s_post, 1)
            pool.wait_ge(s_post, 3)
            pool.memset(V[:, :, :, :, DK:DK + 1], 1.0).then_inc(s_post, 1)
            pool.wait_ge(s_zero, 16)
            pool.wait_ge(s_routed, 1)
            for t in range(NT):
                for j in range(2):
                    pool.indirect_dma_start(slots_x, bass.IndirectOffsetOnAxis(pos[j][:, t:t + 1], 0), rows[:, t, :], None).then_inc(s_scat, 16)
            for par in range(2):
                pool.wait_ge(s_ys[par], 16 * (ET // 2))
            for n in range(HALF):
                if n >= 2:
                    pool.wait_ge(s_cb, n - 1)
                for i, b in enumerate((n, n + HALF)):
                    for q in range(2):
                        for j in range(2):
                            t = 2 * b + q
                            pool.indirect_dma_start(y_tok[n % 2][:, 4 * i + 2 * q + j, :], None, slots_y,
                                                    bass.IndirectOffsetOnAxis(pos[j][:, t:t + 1], 0)).then_inc(s_yg[n % 2], 16)

        @block.scalar
        def _(act):
            act.wait_ge(s_ws, 16)
            act.activation(ws[:, 0, :], ws_stage, ACT.Copy, scale=WS).then_inc(s_hiw, 1)
            act.wait_ge(s_small, 32)
            act.wait_ge(s_d, 1)
            act.activation(tmp[1][:, :], tmp[0][:, :], ACT.Sqrt).then_inc(s_sd, 1)

            def norm(i, a, b):
                if a:
                    act.wait_ge(s_rows, 2 * i + 1)
                    for r in range(2):
                        for j in range(2, 4):
                            t = 8 * i + 4 * r + j
                            ins = act.activation(xn32[r][:, j, :], x[:, bass.ds(t, 1), :].rearrange("p a d -> p (a d)"), ACT.Identity,
                                                 bias=shift[:, bass.ds(t, 1)], scale=rstd[:, bass.ds(t, 1)])
                        ins.then_inc(s_xb, 1)
                if b:
                    for r in range(2):
                        act.wait_ge(s_tr, 2 * i + r - 1)
                        for part in range(2):
                            act.activation(xT[:, part, bass.ds((2 * i - 2 + r) * 4 * P, 4 * P)], bank[2 * r + part][:, :], ACT.Copy).then_inc(s_xt, 1)

            lagged(act, NT // 8, norm)

            act.wait_ge(s_post, NPOST)

            def attend(s, f, k, first_half=True):
                b, par, half = s.at(0)
                ch = chunk_of(s, k, first_half)
                for u in range(8):
                    g = u // 2
                    if f["x"]:
                        for n in (2 * u, 2 * u + 1):
                            act.wait_ge(s_ex, 16 * b + n + 1)
                            if k != 0 or u >= 2:
                                act.wait_ge(s_pv, 8 * b + u - 1)
                            act.activation(A[:, n % 4, :, :].rearrange("p h s -> p (h s)"), EX[n % 2][:, :], ACT.Exp, scale=SCALE).then_inc(s_xp, 1)
                    if u % 2 == 0 and (f["x"] if u else f["o"]):
                        bb, pp, _ = s.at(0 if u else -1)
                        gg = g - 1 if u else 3
                        act.wait_ge(s_pv, 8 * bb + 2 * gg + 2)
                        if gg == 0 and (k is None or bb >= 2):
                            act.wait_ge(s_ot, 2 * bb - 2)
                        act.activation(O[:, pp, gg, :], PV[gg % 2][:, 0:S], ACT.Copy).then_inc(s_pe, 1)
                    if u == 1 and f["x"]:
                        act.wait_ge(s_mt, 2 * b + 2)
                        if k is None or b >= 1:
                            act.wait_ge(s_mr[1 - par][1], 16 * (s.at(-1)[2] + 1))
                        act.activation(mT[:, 1, :, :].rearrange("h q t -> h (q t)"), MISC[1][0:8, 0:S // 2].bitcast(F16), ACT.Copy).then_inc(s_mte, 1)
                        act.wait_ge(s_mte, 2 * b + 2)
                        act.dma_start(stack[ROWS:ROWS + 1, par, 0, 8:16, :], mT[:, 1, :, :].rearrange("h q t -> h (q t)")).then_inc(s_mr[par][1], 16)
                    if u == 0 and f["p"]:
                        b2_, par2, half2 = s.at(2)
                        act.wait_ge(s_qk, b2_ + 1)
                        if k is None or b2_ >= 1:
                            act.wait_ge(s_wr[1 - par2], 144 * (s.at(1)[2] + 1))
                        act.activation(hi_qk[:, :, :].rearrange("p a t -> p (a t)"), MISC[0][:, :], ACT.Copy, scale=1 / WS).then_inc(s_hq, 1)
                    if u == 2 and f["m"]:
                        b1_, par1, _ = s.at(1)
                        act.wait_ge(s_v, b1_ + 1)
                        if f["p"]:
                            act.wait_ge(s_cx, b1_ + 2)
                        if k is None or b1_ >= 2:
                            act.wait_ge(s_pv, 8 * b1_ - 8)
                        act.activation(V[:, par1, :, :, 0:DK], MISC[0][:, S:2 * S].rearrange("p (c h d) -> p c h d", c=2, d=DK), ACT.Copy, scale=1 / WS).then_inc(s_vc, 1)
                    if u == 2 and f["p"]:
                        act.wait_ge(s_cx, b2_ + 1)
                        act.activation(part_c[:, 0, :], MISC[0][0:DE, 0:S], ACT.Copy, scale=CTX / WS).then_inc(s_ch, 1)
                    if u == 4 and f["m"]:
                        b1_, par1, _ = s.at(1)
                        act.wait_ge(s_mt, 2 * b1_ + 1)
                        if k is None or b1_ >= 1:
                            act.wait_ge(s_mr[1 - par1][0], 16 * (s.at(0)[2] + 1))
                        act.activation(mT[:, 0, :, :].rearrange("h q t -> h (q t)"), MISC[0][0:8, 0:S // 2].bitcast(F16), ACT.Copy).then_inc(s_mte, 1)
                        act.wait_ge(s_mte, 2 * b1_ + 1)
                        act.dma_start(stack[ROWS:ROWS + 1, par1, 0, 0:8, :], mT[:, 0, :, :].rearrange("h q t -> h (q t)")).then_inc(s_mr[par1][0], 16)
                    if u == 5 and ch is not None:
                        act.wait_ge(s_wst, 16 * (ch + 1))
                        dst = w12[:, 0, ch * WCH:(ch + 1) * WCH] if isinstance(ch, int) else w12[:, 0, bass.ds(ch * WCH, WCH)]
                        act.activation(dst, w_stage[:, :], ACT.Copy, scale=FS).then_inc(s_whi, 1)
                    if u == 6 and f["o"]:
                        bo = s.at(-1)[0]
                        act.wait_ge(s_oT, bo + 1)
                        if k is None or bo >= 1:
                            act.wait_ge(s_wo, bo)
                        act.activation(oT[:, :], MISC[0][:, 0:2 * P], ACT.Copy).then_inc(s_oTe, 1)
                if k == -2:
                    act.wait_ge(s_sub, 1)
                    act.activation(Ex, Ex, ACT.Exp).then_inc(s_exp8, 1)
                if k == 1:
                    act.wait_ge(s_routed, 1)

            attention_steps(act, 0, attend)

            def expert(quad, r, a, b, c, e, e_before):
                if b:
                    t = 4 * quad + r
                    if not isinstance(t, int) or t >= 2:
                        act.wait_ge(s_fl, 2 * t - 2)
                    for fc in range(FC):
                        act.wait_ge(s_fu, 4 * t + fc + 1)
                        act.activation(h32[r % 2][:, fc, :], bank[fc][:, 0:SLOT], ACT.Gelu_apprx_tanh, bias=b1[:, bass.ds(e + fc, 1)], scale=1 / FS).then_inc(s_fg, 1)

            expert_steps(act, expert, expert_numbers(nc, act, tile_e[0:1, 1, :], FC))
            attention_steps(act, HALF, lambda s, f, k: attend(s, f, k, False))

        @block.vector
        def _(dve):
            chain = [0]

            def link(ins, n=1):
                chain[0] += n
                ins.then_inc(s_d, 1)
                dve.wait_ge(s_d, chain[0])

            def then(ins):
                chain[0] += 1
                ins.then_inc(s_d, 1)

            dve.wait_ge(s_hiw, 1)
            dve.scalar_tensor_tensor(out=ws[:, 1, :], in0=ws_stage, scalar=WS, in1=ws[:, 0, :], op0=ALU.mult, op1=ALU.subtract).then_inc(s_low, 1)
            for q in range(4):
                dve.wait_ge(s_x[q], 16)
                for t in range(q * NT // 4, (q + 1) * NT // 4):
                    ins = dve.bn_stats(stats[:, t, :], x[:, t, :])
                ins.then_inc(s_rd, 1)
            dve.wait_ge(s_rd, NT // 16)
            st = stats
            t0, t1, t2, t3 = (t[:, :] for t in tmp)
            for out_, a, b_, op in ((t1, st[:, :, 1], st[:, :, 4], ALU.add), (t2, st[:, :, 1], st[:, :, 4], ALU.subtract), (t3, st[:, :, 2], st[:, :, 5], ALU.add)):
                ins = dve.tensor_tensor(out_, a, b_, op)
            ins.then_inc(s_rd, 1)
            dve.wait_ge(s_rd, NT // 16 + 1)
            dve.tensor_scalar(mean[:, :], t1, 0.5, None, ALU.mult)
            dve.tensor_tensor(t2, t2, t2, ALU.mult)
            dve.tensor_scalar(t3, t3, 1.0 / D, EPS, ALU.mult, ALU.add).then_inc(s_rd, 1)
            dve.wait_ge(s_rd, NT // 16 + 2)
            link(dve.scalar_tensor_tensor(out=t0, in0=t2, scalar=0.25, in1=t3, op0=ALU.mult, op1=ALU.add))
            dve.wait_ge(s_sd, 1)
            link(dve.reciprocal(t2, t1))
            link(dve.tensor_tensor(t3, t2, t2, ALU.mult))
            link(dve.tensor_tensor(t3, t3, t0, ALU.mult))
            link(dve.tensor_scalar(t3, t3, -0.5, 1.5, ALU.mult, ALU.add))
            link(dve.tensor_tensor(rstd[:, :], t2, t3, ALU.mult))
            dve.scalar_tensor_tensor(out=shift[:, :], in0=mean[:, :], scalar=-1.0, in1=rstd[:, :], op0=ALU.mult, op1=ALU.mult).then_inc(s_rows, 1)
            c0 = chain[0]
            with dve.Fori(0, NT // 8, 1) as i:
                for r in range(2):
                    for j in range(2):
                        t = 8 * i + 4 * r + j
                        ins = dve.tensor_scalar(xn32[r][:, j, :], x[:, bass.ds(t, 1), :].rearrange("p a d -> p (a d)"),
                                                mean[:, bass.ds(t, 1)], rstd[:, bass.ds(t, 1)], ALU.subtract, ALU.mult)
                    ins.then_inc(s_xa, 1)
                for r in range(2):
                    dve.wait_ge(s_xa, 2 * i + r + 1)
                    dve.wait_ge(s_xb, 2 * i + r + 1)
                    dve.tensor_copy(rows[:, bass.ds(8 * i + 4 * r, 4), 0:D], xn32[r]).then_inc(s_d, 1)
                for r in range(2):
                    dve.wait_ge(s_d, 2 * i + c0 + r + 1)
                    dve.tensor_tensor(rows[:, bass.ds(8 * i + 4 * r, 4), D:2 * D], xn32[r], rows[:, bass.ds(8 * i + 4 * r, 4), 0:D], ALU.subtract).then_inc(s_rows, 1)
                dve.wait_ge(s_rows, 2 * i + 3)
            chain[0] += 2 * (NT // 8)
            flat = lambda v: v.rearrange("p t e -> p (t e)")
            dve.wait_ge(s_gate, NT // 4)
            link(dve.tensor_scalar(flat(L), bank[4][:, :], 1 / WS, None, ALU.mult))

            def rank():
                for e in range(NE):
                    won = wins[:, e, :].rearrange("p (t e) -> p t e", e=NE)
                    then(dve.tensor_tensor(won[:, :, 0:e + 1], L[:, :, e:e + 1].to_broadcast([P, NT, e + 1]), L[:, :, 0:e + 1], ALU.is_gt))
                    if e < NE - 1:
                        then(dve.tensor_tensor(won[:, :, e + 1:NE], L[:, :, e:e + 1].to_broadcast([P, NT, NE - 1 - e]), L[:, :, e + 1:NE], ALU.is_ge))
                then(dve.tensor_reduce(tmp[0][:, :], L, AX.X, ALU.max))
                dve.wait_ge(s_d, chain[0])
                dve.tensor_tensor(Ex, L, tmp[0][:, :].unsqueeze(2).to_broadcast([P, NT, NE]), ALU.subtract).then_inc(s_sub, 1)
                n = NE
                while n > 2:
                    n //= 2
                    link(dve.tensor_tensor(wins[:, 0:n, :], wins[:, 0:n, :], wins[:, n:2 * n, :], ALU.add))
                link(dve.tensor_tensor(flat(Ta), wins[:, 0, :], wins[:, 1, :], ALU.add))
                dve.tensor_scalar(picked[:, :], flat(Ta), 2.0, None, ALU.is_lt).then_inc(s_m, 1)
                for j in range(2):
                    link(dve.tensor_scalar(flat(sel[j]), flat(Ta), float(j), None, ALU.is_equal))

            def slots():
                dve.wait_ge(s_cnt, 1)
                link(dve.tensor_copy(flat(scan[0]), bank[4][:, :]))
                link(dve.tensor_copy(flat(Ta), flat(scan[0])))
                dve.tensor_copy(flat(before_tok), bank[5][:, :]).then_inc(s_cntr, 1)
                dve.wait_ge(s_cntr, 1)
                yield
                dve.wait_ge(s_exp8, 1)
                link(dve.tensor_reduce(tmp[0][:, :], Ex, AX.X, ALU.add))
                link(dve.reciprocal(tmp[1][:, :], tmp[0][:, :]))
                yield
                for j in range(2):
                    link(dve.tensor_tensor(Tb, Ex, sel[j], ALU.mult))
                    link(dve.tensor_reduce(tmp[2][:, :], Tb, AX.X, ALU.add))
                    link(dve.tensor_tensor(prob[j][:, :], tmp[2][:, :], tmp[1][:, :], ALU.mult))
                    yield
                src, dst, d = scan[0], scan[1], 1
                while d < NT:
                    then(dve.tensor_copy(dst[:, 0:d, :], src[:, 0:d, :]))
                    link(dve.tensor_tensor(dst[:, d:NT, :], src[:, d:NT, :], src[:, 0:NT - d, :], ALU.add))
                    src, dst, d = dst, src, 2 * d
                    yield
                link(dve.tensor_scalar(cnt8i[:, :], src[:, NT - 1, :], float(SLOT - 1), None, ALU.add))
                link(dve.tensor_single_scalar(cnt8i[:, :], cnt8i[:, :], SLOT.bit_length() - 1, op=ALU.logical_shift_right))
                link(dve.tensor_copy(cnt8[:, 0, :], cnt8i[:, :]))
                link(dve.tensor_copy(cnt8[:, 1, :], cnt8[:, 0, :]))
                yield
                for e in range(1, NE):
                    link(dve.tensor_tensor(cnt8[:, 1, e:e + 1], cnt8[:, 1, e - 1:e], cnt8[:, 0, e:e + 1], ALU.add))
                    if e % 4 == 0:
                        yield
                link(dve.tensor_tensor(cnt8[:, 2, :], cnt8[:, 1, :], cnt8[:, 0, :], ALU.subtract))
                link(dve.tensor_scalar(cnt8[:, 3, :], cnt8[:, 2, :], float(SLOT), None, ALU.mult))
                yield
                link(dve.tensor_tensor(dst, src, Ta, ALU.subtract))
                link(dve.tensor_tensor(Ta, before_tok, dst, ALU.add))
                yield
                link(dve.tensor_tensor(Ta, Ta, cnt8[:, 3, :].unsqueeze(1).to_broadcast([P, NT, NE]), ALU.add))
                for j in range(2):
                    link(dve.tensor_tensor(Tb, Ta, sel[j], ALU.mult))
                    yield
                    link(dve.tensor_reduce(tmp[2][:, :], Tb, AX.X, ALU.add))
                    link(dve.tensor_copy(pos[j][:, :], tmp[2][:, :]))
                n = ET + 4
                tf = tile_f[:, 0:n * NE].rearrange("p (t e) -> p t e", e=NE)
                te = tile_f[:, n * NE:n * NE + n].rearrange("p (q j) -> p q j", j=4)
                word = tile_f[:, n * (NE + 1):]
                link(dve.tensor_copy(tf, tile_no[:, :].unsqueeze(2).to_broadcast([1, n, NE])))
                yield
                link(dve.tensor_tensor(tf, tf, cnt8[0:1, 1, :].unsqueeze(1).to_broadcast([1, n, NE]), ALU.is_ge))
                link(dve.tensor_reduce(te.rearrange("p q j -> p (q j)"), tf, AX.X, ALU.add))
                yield
                link(dve.tensor_scalar(te, te, float(NE - 1), None, ALU.min))
                acc = te[:, 1:1 + ET // 4, 0]
                for j in (3, 2, 1, 0):
                    link(dve.scalar_tensor_tensor(out=word, in0=acc, scalar=float(2 ** DIGIT), in1=te[:, 0:ET // 4, j], op0=ALU.mult, op1=ALU.add))
                    acc = word
                link(dve.tensor_scalar(tile_e[:, 0, :], word, float(FF), None, ALU.mult))
                dve.tensor_scalar(tile_e[:, 1, :], word, float(FC), None, ALU.mult).then_inc(s_routed, 1)

            pieces = slots()
            c_rd = NT // 16 + 2

            def combine(s, n):
                bc, par, half = s.at(-2)
                j, i = n // 2, n % 2
                if n == 0:
                    dve.wait_ge(s_yg[par], 128 * (half - HALF // 2 + 1))
                    dve.wait_ge(s_acc, bc + 1)
                if n == 2:
                    dve.wait_ge(s_c1, bc - HALF + 1)
                for q in range(2):
                    t = 2 * (bc - HALF * (1 - i)) + q
                    if isinstance(t, int):
                        xx, pr = x[:, t, :], prob[j][:, t:t + 1]
                    else:
                        xx, pr = x[:, bass.ds(t, 1), :].rearrange("p a d -> p (a d)"), prob[j][:, bass.ds(t, 1)]
                    ins = dve.scalar_tensor_tensor(out=xx, in0=y_tok[par][:, 4 * i + 2 * q + j, :], scalar=pr, in1=xx, op0=ALU.mult, op1=ALU.add)
                if i == 1:
                    ins.then_inc((s_c1, s_cb)[j], 1)

            def attend(s, f, k, first_half=True):
                b, par, half = s.at(0)
                b1_, par1, half1 = s.at(1)
                ch = chunk_of(s, k, first_half)
                for u in range(8):
                    if first_half and k == -2 and u == 3:
                        rank()
                    if first_half and k in (-1, 0, 1):
                        next(pieces, None)
                    if f["m"]:
                        g, qt = u // 2, u % 2
                        for p in range(2):
                            n = 2 * u + p
                            dve.wait_ge(s_mx, 16 * b1_ + n + 1)
                            dve.tensor_reduce(mx[:, par1, qt, 4 * g + 2 * p:4 * g + 2 * p + 2], MX[p][:, :].rearrange("q (h k) -> q h k", h=2), AX.X, ALU.max).then_inc(s_red, 1)
                        if u in (3, 7):
                            a = u // 4
                            dve.wait_ge(s_red, 16 * b1_ + 8 * a + 8)
                            if k is None or b1_ >= 1:
                                dve.wait_ge(s_mt, 2 * b1_ + a - 1)
                            dve.tensor_scalar(negm[:, a, :, :], mx[:, par1, :, 8 * a:8 * a + 8], -1.0, None, ALU.mult).then_inc(s_nm, 1)
                    if u == 0 and f["c"]:
                        bc = s.at(-2)[0]
                        dve.wait_ge(s_wo, bc + 1)
                        xs_ = x[:, 2 * bc:2 * bc + 2, :] if isinstance(bc, int) else x[:, bass.ds(2 * bc, 2), :]
                        dve.tensor_tensor(xs_, xs_, MISC[1][:, 0:2 * P].rearrange("p (q d) -> p q d", q=2), ALU.add).then_inc(s_acc, 1)
                    if 1 <= u <= 4 and f["c"] and not first_half:
                        combine(s, u - 1)
                    if u == 0 and f["p"]:
                        b2_ = s.at(2)[0]
                        dve.wait_ge(s_hq, b2_ + 1)
                        dve.scalar_tensor_tensor(out=lo_qk[:, :, :].rearrange("p a t -> p (a t)"), in0=MISC[0][:, :], scalar=1 / WS,
                                                 in1=hi_qk[:, :, :].rearrange("p a t -> p (a t)"), op0=ALU.mult, op1=ALU.subtract).then_inc(s_lq, 1)
                    if u == 2 and f["p"]:
                        dve.wait_ge(s_ch, b2_ + 1)
                        dve.scalar_tensor_tensor(out=part_c[:, 1, :], in0=MISC[0][0:DE, 0:S], scalar=CTX / WS, in1=part_c[:, 0, :],
                                                 op0=ALU.mult, op1=ALU.subtract).then_inc(s_cl, 1)
                    if u in (3, 5) and f["o"]:
                        bo = s.at(-1)[0]
                        qt = (u - 3) // 2
                        dve.wait_ge(s_ot, 2 * bo + qt + 1)
                        v = MISC[1][:, :].rearrange("q (h r) -> q h r", r=32)
                        dve.reciprocal(rden[:, qt, :], v[:, :, DK]).then_inc(s_rd, 1)
                        dve.wait_ge(s_rd, 2 * bo + qt + 1 + c_rd)
                        if qt == 0 and (k is None or bo >= 1):
                            dve.wait_ge(s_oT, bo)
                        dve.tensor_tensor(o_n[:, qt, :, :], v[:, :, 0:DK], rden[:, qt, :].unsqueeze(2).to_broadcast([P, H, DK]), ALU.mult).then_inc(s_on, 1)
                    if u == 6 and ch is not None:
                        dve.wait_ge(s_whi, ch + 1)
                        hi, lo = ((w12[:, part, ch * WCH:(ch + 1) * WCH] if isinstance(ch, int) else w12[:, part, bass.ds(ch * WCH, WCH)]) for part in range(2))
                        dve.scalar_tensor_tensor(out=lo, in0=w_stage[:, :], scalar=FS, in1=hi, op0=ALU.mult, op1=ALU.subtract).then_inc(s_wlo, 1)

            attention_steps(dve, 0, attend)
            assert next(pieces, None) is None
            dve.wait_ge(s_b2, 16)

            def expert(quad, r, a, b, c, e, e_before):
                t = 4 * quad + r
                static = isinstance(t, int)
                if a:
                    n, par = t + 1, (r + 1) % 2
                    dve.wait_ge(s_ft, n + 1)
                    if not static or n >= 2:
                        dve.wait_ge(s_fu, 4 * n - 4)
                    dve.tensor_copy(xt[par].rearrange("p a s -> p (a s)"), bank[4 + par][:, 0:SLOT].bitcast(F16)).then_inc(s_fx, 1)
                if b:
                    par = r % 2
                    for hf in range(2):
                        dve.wait_ge(s_fg, 4 * t + 2 * hf + 2)
                        if hf == 0 and (not static or t >= 2):
                            dve.wait_ge(s_fd, t - 1)
                        hi, lo, h = (v[:, 2 * hf:2 * hf + 2, :] for v in (hp[par][:, 0], hp[par][:, 1], h32[par]))
                        dve.tensor_copy(hi, h).then_inc(s_fh, 1)
                        dve.wait_ge(s_fh, 2 * t + hf + 1)
                        dve.tensor_tensor(lo, h, hi, ALU.subtract).then_inc(s_fl, 1)
                if c:
                    n, par = t - 1, (r - 1) % 2
                    dve.wait_ge(s_fd, n + 1)
                    if not static or n >= 2:
                        dve.wait_ge(s_ys[par], 16 * (2 * quad + (r - 1) // 2))
                    dve.scalar_tensor_tensor(out=ye[par], in0=bank[6 + par][:, 0:2 * D].rearrange("p (s d) -> p s d", s=2), scalar=1 / FS,
                                             in1=b2[:, bass.ds(e_before * (D // FC), D)].unsqueeze(1).to_broadcast([P, 2, D]), op0=ALU.mult, op1=ALU.add).then_inc(s_fy, 1)

            expert_steps(dve, expert, expert_numbers(nc, dve, tile_e[0:1, 1, :], FC))

            attention_steps(dve, HALF, lambda s, f, k: attend(s, f, k, False))

        @block.tensor
        def _(pe):
            pe.wait_ge(s_const, NCONST)
            pe.wait_ge(s_low, 1)

            def norm(i, a, b):
                if a:
                    for r in range(2):
                        pe.wait_ge(s_rows, 2 * i + r + 2)
                        if not isinstance(i, int):
                            pe.wait_ge(s_xt, 4 * i + 2 * r - 2)
                        for part in range(2):
                            for j in range(4):
                                t = 8 * i + 4 * r + j
                                mm = pe.matmul(bank[2 * r + part][:, j * P:(j + 1) * P], rows[:, bass.ds(t, 1), part * D:(part + 1) * D].rearrange("p a d -> p (a d)"),
                                               ident16[:, :], start=True, stop=True)
                        mm.then_inc(s_tr, 1)
                if b:
                    for r in range(2):
                        pe.wait_ge(s_xt, 4 * i + 2 * r - 2)
                        for j in range(4):
                            t = 8 * i - 8 + 4 * r + j
                            for n, (pa, pb) in enumerate(TERMS):
                                mm = pe.matmul(bank[4][:, bass.ds(t * NE, NE)], xT[:, pa, bass.ds(t * P, P)], ws[:, pb, CG:CG + NE], start=(n == 0), stop=(n == 2))
                        mm.then_inc(s_gate, 1)

            lagged(pe, NT // 8, norm)

            def drained(e, s, f, k):
                def readers(e, off, f, k):
                    n = lambda o: s.at(off + o)[0]
                    return {0: f["p"] and [(s_lq, n(2) + 1)], 1: f["x"] and [(s_mte, 2 * n(0) + 2)],
                            2: (f["p"] or f["m"]) and [(s_cl, n(2) + 1)] * f["p"] + [(s_vc, n(1) + 1)] * f["m"],
                            3: f["o"] and [(s_on, 2 * n(-1) + 1)], 4: f["m"] and [(s_mte, 2 * n(1) + 1)],
                            5: f["o"] and [(s_on, 2 * n(-1) + 2)], 6: f["o"] and [(s_oTe, n(-1) + 1)],
                            7: f["o"] and [(s_acc, n(-1) + 1)]}[e]
                off, ee = 0, e - 2
                while True:
                    if ee < 0:
                        ee += 8
                        off -= 1
                        if k is not None:
                            if off < -2:
                                return
                            f = attention_flags(k + off, HALF * phase[0])
                    got = readers(ee, off, f, k)
                    if got:
                        for sm, v in got:
                            if not isinstance(v, int) or v > 0:
                                pe.wait_ge(sm, v)
                        return
                    ee -= 2

            phase = [0]

            def xcols(part, b, n=S, o=0):
                return xT[:, part, b * S + o:b * S + o + n] if isinstance(b, int) else xT[:, part, bass.ds(b * S + o, n)]

            def attend(s, f, k):
                b, par, half = s.at(0)
                b1_, par1, half1 = s.at(1)
                b2_ = s.at(2)[0]
                bo, paro, _ = s.at(-1)

                def values(bb, pp, v):
                    g, c = v // 2, v % 2
                    pe.wait_ge(s_xp, 16 * bb + 2 * v + 2)
                    if v == 0:
                        pe.wait_ge(s_vc, bb + 1)
                    if c == 0 and (not isinstance(bb, int) or 4 * bb + g >= 2):
                        pe.wait_ge(s_pe, 4 * bb + g - 1)
                    for i in range(4):
                        mm = pe.matmul(PV[g % 2][32 * i:32 * i + 32, 0:S], V[:, pp, c, 4 * g + i, :], A[:, (2 * v + i // 2) % 4, i % 2, :],
                                       start=(c == 0), stop=(c == 1))
                    mm.then_inc(s_pv, 1)

                for u in range(8):
                    g, c = u // 2, u % 2
                    if f["x"]:
                        if u in (0, 4):
                            pe.wait_ge(s_mr[par][u // 4], 16 * (half + 1))
                        for p in range(2):
                            n = 2 * u + p
                            if not isinstance(b, int) or 16 * b + n >= 2:
                                pe.wait_ge(s_xp, 16 * b + n - 1)
                            for i in range(2):
                                h = 4 * g + 2 * p + i
                                mm = pe.matmul(EX[p][:, i * S:(i + 1) * S], stack[0:ROWS + 1, par, 1, h, c * P:(c + 1) * P], stack[0:ROWS + 1, par, 0, h, :], start=True, stop=True)
                            mm.then_inc(s_ex, 1)
                    if f["m"]:
                        if c == 0:
                            if g % 2 == 0:
                                pe.wait_ge(s_st[par1][g // 2], 64 * (half1 + 1))
                        for p in range(2):
                            n = 2 * u + p
                            if not isinstance(b1_, int) or 16 * b1_ + n >= 2:
                                pe.wait_ge(s_red, 16 * b1_ + n - 1)
                            for i in range(2):
                                h = 4 * g + 2 * p + i
                                mm = pe.matmul(MX[p][:, i * S:(i + 1) * S], stack[0:ROWS, par1, 0, h, c * P:(c + 1) * P], stack[0:ROWS, par1, 1, h, :], start=True, stop=True)
                            mm.then_inc(s_mx, 1)
                    if u == 0 and f["o"]:
                        values(bo, paro, 7)
                    if u > 0 and f["x"]:
                        values(b, par, u - 1)
                    M = MISC[u % 2]
                    if (u == 1 and f["x"]) or (u == 4 and f["m"]):
                        a = 1 if u == 1 else 0
                        drained(u, s, f, k)
                        pe.wait_ge(s_nm, 2 * (b if u == 1 else b1_) + a + 1)
                        for q in range(2):
                            mm = pe.transpose(M[0:8, 0:S // 2].bitcast(F16)[:, q * P:(q + 1) * P], negm[:, a, q, :], ident16[:, :])
                        mm.then_inc(s_mt, 1)
                    if u == 0 and f["p"]:
                        drained(u, s, f, k)
                        for side, col in ((0, CQ), (1, CK)):
                            for n, (pa, pb) in enumerate(TERMS):
                                mm = pe.matmul(M[:, side * S:(side + 1) * S], ws[:, pa, col:col + D], xcols(pb, b2_), start=(n == 0), stop=(n == 2))
                        mm.then_inc(s_qk, 1)
                    if u == 2 and (f["p"] or f["m"]):
                        drained(u, s, f, k)
                        if f["m"]:
                            for q in range(2):
                                for n, (pa, pb) in enumerate(TERMS):
                                    mm = pe.matmul(M[:, S + q * P:S + (q + 1) * P], xcols(pa, b1_, P, q * P), ws[:, pb, CV:CV + D], start=(n == 0), stop=(n == 2))
                            mm.then_inc(s_v, 1)
                        if f["p"]:
                            for n, (pa, pb) in enumerate(TERMS):
                                mm = pe.matmul(M[0:DE, 0:S], ws[:, pa, CE:CE + DE], xcols(pb, b2_), start=(n == 0), stop=(n == 2))
                            mm.then_inc(s_cx, 1)
                    if u in (3, 5) and f["o"]:
                        drained(u, s, f, k)
                        qt = (u - 3) // 2
                        if qt == 0:
                            pe.wait_ge(s_pe, 4 * bo + 4)
                        for gg in range(4):
                            mm = pe.transpose(M[:, gg * P:(gg + 1) * P], O[:, paro, gg, qt * P:(qt + 1) * P], ident[:, :])
                        mm.then_inc(s_ot, 1)
                    if u == 6 and f["o"]:
                        drained(u, s, f, k)
                        pe.wait_ge(s_on, 2 * bo + 2)
                        for q in range(2):
                            mm = pe.transpose(M[:, q * P:(q + 1) * P], o_n[:, q, :, :].rearrange("p h d -> p (h d)"), ident[:, :])
                        mm.then_inc(s_oT, 1)
                    if u == 7 and f["o"]:
                        drained(u, s, f, k)
                        pe.wait_ge(s_oTe, bo + 1)
                        for q in range(2):
                            mm = pe.matmul(M[:, q * P:(q + 1) * P], oT[:, q * P:(q + 1) * P], wo[:, :], start=True, stop=True)
                        mm.then_inc(s_wo, 1)
                if k == -2:
                    pe.wait_ge(s_m, 1)
                    pe.matmul(bank[5][:, :], before[:, :], picked[:, :], start=True, stop=True)
                    pe.matmul(bank[4][:, :], ones16[:, :], picked[:, :], start=True, stop=True).then_inc(s_cnt, 1)
                if k == -1:
                    pe.wait_ge(s_cntr, 1)

            attention_steps(pe, 0, attend)
            for sm, n in ((s_red, 16 * (HALF + 1)), (s_xp, 16 * HALF), (s_pe, 4 * HALF), (s_vc, HALF + 1), (s_lq, HALF + 2), (s_cl, HALF + 2), (s_oTe, HALF), (s_acc, HALF), (s_wlo, NCH), (s_routed, 1)):
                pe.wait_ge(sm, n)

            def expert(quad, r, a, b, c, e, e_before):
                t = 4 * quad + r
                static = isinstance(t, int)
                if a:
                    n, par, r4 = t + 1, (r + 1) % 2, (r + 1) % 4
                    pe.wait_ge(s_xr[r4], 16 * (quad + (r + 1) // 4 + 1))
                    if not static or n >= 2:
                        pe.wait_ge(s_fx, n - 1)
                    v = bank[4 + par][:, 0:SLOT].bitcast(F16)
                    for part in range(2):
                        for h in range(2):
                            mm = pe.transpose(v[:, part * SLOT + h * P:part * SLOT + (h + 1) * P], xr[r4][:, h, part * D:(part + 1) * D], ident16[:, :])
                    mm.then_inc(s_ft, 1)
                if b:
                    pe.wait_ge(s_fx, t + 1)
                    for fc in range(FC):
                        if not static or t >= 1:
                            pe.wait_ge(s_fg, 4 * t + fc - 3)
                        for n, (pa, pb) in enumerate(TERMS):
                            mm = pe.matmul(bank[fc][:, 0:SLOT], w1[:, pa, bass.ds(e + fc * P, P)], xt[r % 2][:, pb, :], start=(n == 0), stop=(n == 2))
                        mm.then_inc(s_fu, 1)
                if c:
                    n, par = t - 1, (r - 1) % 2
                    pe.wait_ge(s_fl, 2 * n + 2)
                    if not static or n >= 2:
                        pe.wait_ge(s_fy, n - 1)
                    for h in range(2):
                        for fc in range(FC):
                            for m, (pa, pb) in enumerate(TERMS):
                                mm = pe.matmul(bank[6 + par][:, h * D:(h + 1) * D], hp[par][:, pa, fc, h * P:(h + 1) * P], w2[:, pb, bass.ds(e_before + fc * P, P)],
                                               start=(fc == 0 and m == 0), stop=(fc == FC - 1 and m == 2))
                    mm.then_inc(s_fd, 1)

            expert_steps(pe, expert, expert_numbers(nc, pe, tile_e[0:1, 0, :], FF))
            for sm, n in ((s_fy, ET), (s_fg, FC * ET), (s_fx, ET)):
                pe.wait_ge(sm, n)
            phase[0] = 1
            attention_steps(pe, HALF, attend)


def kernel(L0_attn_X, L0_attn_Wq, L0_attn_Wk, L0_attn_Wv, L0_attn_Wo, L0_attn_We, L0_ffn_gate_w, L0_ffn_w1, L0_ffn_b1, L0_ffn_w2, L0_ffn_b2):
    import numpy as np
    import concourse.bacc as bacc
    from concourse.bass_utils import run_bass_kernel_spmd

    turned = [np.asarray(w).T for w in (L0_attn_Wq, L0_attn_Wk, L0_attn_Wv, L0_attn_We, L0_ffn_gate_w)]
    w2 = np.asarray(L0_ffn_w2).transpose(1, 2, 0).reshape(NE, FC, P, D).transpose(2, 0, 1, 3).reshape(P, NE * FF)
    w1 = np.asarray(L0_ffn_w1).transpose(2, 1, 0).reshape(D, NE * FF)
    arrays = {
        "x": np.asarray(L0_attn_X).reshape(B * S, D),
        "wsmall": np.concatenate(turned, axis=1),
        "wo": np.asarray(L0_attn_Wo).T,
        "w12": np.concatenate([w1, w2], axis=1),
        "b1": np.asarray(L0_ffn_b1).reshape(NE * FC, P).T,
        "b2": np.asarray(L0_ffn_b2).reshape(1, NE * D),
    }
    arrays = {f"in_{n}": np.ascontiguousarray(a) for n, a in arrays.items()}
    nc = bacc.Bacc("TRN2", target_bir_lowering=False, num_devices=1)
    ins = [nc.dram_tensor(n, list(a.shape), mybir.dt.from_np(a.dtype), kind="ExternalInput").ap() for n, a in arrays.items()]
    out = nc.dram_tensor("out_rows", [B * S, D], F32, kind="ExternalOutput").ap()
    build(nc, *ins, out)
    r = run_bass_kernel_spmd(nc, [arrays], core_ids=[0])
    return np.asarray(r.results[0]["out_rows"]).reshape(B, S, D)
```

```python
from contextlib import ExitStack

import concourse.bass as bass
from concourse import mybir

F32 = mybir.dt.float32
F16 = mybir.dt.float16
I32 = mybir.dt.int32
U32 = mybir.dt.uint32
ALU = mybir.AluOpType
ACT = mybir.ActivationFunctionType
AX = mybir.AxisListType

P = 128
D = 128
B = 32
S = 256
H = 16
DK = D // H
DE = D // 8
NE = 8
FF = 512
FC = FF // P
NT = B * S // P
EPS = 1e-5
SLOT = 256
ET = -(-(2 * B * S) // SLOT) + NE
UNROLL = 8
DIGIT = 3
ROWS = 3 * DK + 3 * DE
WCH = 1024
WS = 2.0 ** 8
FS = 2.0 ** 10
SCALE = DK ** -0.5
CTX = (0.1 / SCALE) ** 0.5
HALF = B // 2
NW = 3 * D + DE + NE
CQ, CK, CV, CE, CG = 0, D, 2 * D, 3 * D, 3 * D + DE
TERMS = ((0, 0), (0, 1), (1, 0))


class Step:

    def __init__(self, half, r):
        self.half, self.r = half, r

    def at(self, off):
        n = self.r + off
        return 2 * self.half + n, n % 2, self.half + n // 2


def attention_flags(k, b0):
    first, last = (0, HALF - 1) if b0 == 0 else (b0, B - 1)
    ahead = {"p": 2, "m": 1}
    return {s: first + (ahead.get(s, 0) if b0 else 0) <= k + off <= last + (0 if b0 else ahead.get(s, 0))
            for s, off in (("p", 2), ("m", 1), ("x", 0), ("o", -1), ("c", -2))}


ALL = dict.fromkeys("pmxoc", True)


def attention_steps(eng, b0, body):
    for k in range(b0 if b0 else -2, b0 + 2):
        body(Step(k // 2, k % 2), attention_flags(k, b0), k)
    with eng.Fori(b0 // 2 + 1, b0 // 2 + HALF // 2 - 1, 1) as half:
        for r in range(2):
            body(Step(half, r), ALL, None)
    for k in range(b0 + HALF - 2, b0 + HALF + 2):
        body(Step(k // 2, k % 2), attention_flags(k, b0), k)


def lagged(eng, n, body, end=True):
    body(0, True, False)
    with eng.Fori(1, n, 1) as i:
        body(i, True, True)
    if end:
        body(n, False, True)


def expert_steps(eng, body, load=None):
    last = 5 + UNROLL * ((ET - 7) // UNROLL)
    load = load or (lambda n, count: [None] * count)
    e = load(0, 5)
    for t in range(-1, 5):
        body(t // 4, t % 4, t + 1 < ET, t >= 0, t >= 1, e[max(t, 0)], e[max(t - 1, 0)])
    with eng.Fori(0, (last - 5) // UNROLL, 1) as i:
        quad = UNROLL // 4 * i + 1
        e = load(quad, UNROLL + 1)
        for r in range(1, UNROLL + 1):
            body(quad, r, True, True, True, e[r], e[r - 1])
    e = load((last - 1) // 4, ET - last + 1)
    for t in range(last, ET + 1):
        body(t // 4, t % 4, t + 1 < ET, t < ET, True, e[min(t, ET - 1) - last + 1], e[t - last])


def expert_numbers(nc, eng, words, unit):
    def load(quad, count):
        nw = max((count - 1) // 4, 1)
        word = nc.values_load_multi_w_load_instructions(words[:, bass.ds(quad, nw)], engines=[eng.engine], min_val=0, max_val=(NE ** 5 - 1) * unit)[1]
        digits = [(min(j // 4, nw - 1), j) for j in range(count)]
        return [eng.snap((word[w] >> (DIGIT * (j - 4 * w))) & ((NE - 1) * unit)) for w, j in digits]
    return load


def build(nc, X, Wsmall, Wo, W12, B1, B2, out):
    with ExitStack() as ctx:
        def sb(name, shape, dt):
            return ctx.enter_context(nc.sbuf_tensor(name, shape, dt))

        def sem(name):
            return ctx.enter_context(nc.semaphore(name))

        slots_x = nc.dram_tensor("slots_x", [ET * SLOT, 2 * D], F16, kind="Internal").ap()
        slots_y = nc.dram_tensor("slots_y", [ET * SLOT, D], F32, kind="Internal").ap()
        qk_dram = nc.dram_tensor("qk_dram", [2, 2, 3 * DK, H * S], F16, kind="Internal").ap()
        ctx_dram = nc.dram_tensor("ctx_dram", [2, 5 * DE, S], F16, kind="Internal").ap()

        x = sb("x", [P, NT, D], F32)
        rows = sb("rows", [P, NT, 2 * D], F16)
        xT = sb("xT", [P, 2, B * S], F16)
        w12 = sb("w12", [P, 2, 2 * NE * FF], F16)
        w_stage = sb("w_stage", [P, WCH], F32)
        w1, w2 = w12[:, :, 0:NE * FF], w12[:, :, NE * FF:2 * NE * FF]
        ws = sb("ws", [P, 2, NW], F16)
        wo = sb("wo", [P, D], F32)
        b1 = sb("b1", [P, NE * FC], F32)
        stack = sb("stack", [P, 2, 2, H, S], F16)
        A = sb("A", [P, 4, 2, S], F32)
        V = sb("V", [P, 2, 2, H, 32], F32)
        O = sb("O", [P, 2, 4, S], F32)
        hi_qk = sb("hi_qk", [P, 2, S], F16)
        lo_qk = sb("lo_qk", [P, 2, S], F16)
        part_c = sb("part_c", [DE, 2, S], F16)
        mx = sb("mx", [P, 2, 2, H], F32)
        negm = sb("negm", [P, 2, 2, 8], F16)
        mT = sb("mT", [8, 2, 2, P], F16)
        rden = sb("rden", [P, 2, H], F32)
        o_n = sb("o_n", [P, 2, H, DK], F32)
        oT = sb("oT", [P, 2 * P], F32)
        ident = sb("ident", [P, P], F32)
        ident16 = sb("ident16", [P, P], F16)
        before = sb("before", [P, P], F16)
        ones16 = sb("ones16", [P, P], F16)
        zeros = sb("zeros", [P, 2 * D], F16)
        stats = sb("stats", [P, NT, 6], F32)
        mean = sb("mean", [P, NT], F32)
        rstd = sb("rstd", [P, NT], F32)
        shift = sb("shift", [P, NT], F32)
        tmp = [sb(f"tmp{i}", [P, NT], F32) for i in range(4)]
        prob = [sb(f"prob{i}", [P, NT], F32) for i in range(2)]
        pos = [sb(f"pos{i}", [P, NT], U32) for i in range(2)]
        picked = sb("picked", [P, NT * NE], F16)
        cnt8 = sb("cnt8", [P, 4, NE], F32)
        tile_no = sb("tile_no", [1, ET + 4], I32)
        tile_e = sb("tile_e", [1, 2, ET // 4], I32)

        early = w12[:, :, :].rearrange("p a n -> p (a n)")
        taken = [0]

        def temp(n):
            taken[0] += 2 * n
            return early[:, taken[0] - 2 * n:taken[0]].bitcast(F32)

        xn32 = [temp(4 * D).rearrange("p (j d) -> p j d", d=D) for _ in range(2)]
        ws_stage = temp(NW)
        L, Ex, Ta, Tb, scan0, scan1, sel0, sel1, before_tok = (temp(NT * NE).rearrange("p (t e) -> p t e", e=NE) for _ in range(9))
        scan, sel = (scan0, scan1), (sel0, sel1)
        wins32 = temp(NE * NT * NE // 2)
        wins = wins32.bitcast(F16).rearrange("p (a n) -> p a n", a=NE)
        tile_f = wins32[0:1, 0:(ET + 4) * (NE + 1) + ET // 4]
        assert taken[0] <= 4 * NE * FF
        free = rows[:, :, :].rearrange("p t d -> p (t d)")
        at = [0]

        def carve(n, dt):
            v = free[:, at[0]:at[0] + n * (2 if dt == F32 else 1)]
            at[0] += n * (2 if dt == F32 else 1)
            return v.bitcast(F32) if dt == F32 else v

        xr = [carve(2 * 2 * D, F16).rearrange("p (s c) -> p s c", s=2) for _ in range(4)]
        xt = [carve(2 * SLOT, F16).rearrange("p (a s) -> p a s", a=2) for _ in range(2)]
        h32 = [carve(FC * SLOT, F32).rearrange("p (f s) -> p f s", f=FC) for _ in range(2)]
        hp = [carve(2 * FC * SLOT, F16).rearrange("p (a f s) -> p a f s", a=2, f=FC) for _ in range(2)]
        ye = [carve(2 * D, F32).rearrange("p (s d) -> p s d", s=2) for _ in range(2)]
        b2 = carve(NE * D, F32)
        assert at[0] <= NT * 2 * D
        at[0] = 0
        y_tok = [carve(8 * D, F32).rearrange("p (j d) -> p j d", j=8) for _ in range(2)]

        bank = [ctx.enter_context(nc.psum_tensor(f"bank{i}", [P, 512], F32)) for i in range(8)]
        MX, EX, PV, MISC = (bank[0], bank[1], bank[5]), bank[2:4], bank[4], bank[6:8]
        MX_ORDER = [n % 3 for n in range(15)] + [1]

        def mx_read(n):
            earlier = [m for m in range(-16, n) if MX_ORDER[m % 16] == MX_ORDER[n]]
            return earlier[-1] + 1

        s_x = [sem(f"s_x{q}") for q in range(4)]
        s_ws, s_small, s_wst, s_b2 = sem("s_ws"), sem("s_small"), sem("s_wst"), sem("s_b2")
        s_xa, s_xb, s_whi, s_wlo, s_cntr = (sem(n) for n in ("s_xa", "s_xb", "s_whi", "s_wlo", "s_cntr"))
        s_pd, s_pos, s_ysum = sem("s_pd"), sem("s_pos"), sem("s_ysum")
        s_const, s_zero, s_post = sem("s_const"), sem("s_zero"), sem("s_post")
        s_hiw, s_low = sem("s_hiw"), sem("s_low")
        s_d, s_sd, s_rows, s_tr, s_xt, s_gate = (sem(n) for n in ("s_d", "s_sd", "s_rows", "s_tr", "s_xt", "s_gate"))
        s_sub, s_exp8, s_m, s_cnt, s_routed, s_scat = (sem(n) for n in ("s_sub", "s_exp8", "s_m", "s_cnt", "s_routed", "s_scat"))
        s_qk, s_hq, s_lq, s_cx, s_ch, s_cl, s_v, s_vc = (sem(n) for n in ("s_qk", "s_hq", "s_lq", "s_cx", "s_ch", "s_cl", "s_v", "s_vc"))
        s_wr = [sem(f"s_wr{i}") for i in range(2)]
        s_st = [[sem(f"s_st{i}_{g}") for g in range(2)] for i in range(2)]
        s_mr = [[sem(f"s_mr{i}_{a}") for a in range(2)] for i in range(2)]
        s_mx, s_red, s_nm, s_mt, s_mte = (sem(n) for n in ("s_mx", "s_red", "s_nm", "s_mt", "s_mte"))
        s_ex, s_xp, s_pv, s_pe = (sem(n) for n in ("s_ex", "s_xp", "s_pv", "s_pe"))
        s_ot, s_rd, s_on, s_oT, s_oTe, s_wo, s_acc = (sem(n) for n in ("s_ot", "s_rd", "s_on", "s_oT", "s_oTe", "s_wo", "s_acc"))
        s_xr = [sem(f"s_xr{i}") for i in range(4)]
        s_ft, s_fx, s_fu, s_fg, s_fh, s_fl, s_fd, s_fy = (sem(n) for n in ("s_ft", "s_fx", "s_fu", "s_fg", "s_fh", "s_fl", "s_fd", "s_fy"))
        s_ys = [sem(f"s_ys{i}") for i in range(2)]
        s_yg = [sem(f"s_yg{i}") for i in range(2)]
        s_c1, s_cb, s_out = sem("s_c1"), sem("s_cb"), sem("s_out")

        block = ctx.enter_context(nc.Block())
        NCONST, NPOST, NRANK = 10, 4, 37
        NCH = 2 * NE * FF // WCH

        def chunk_of(s, k, first_half):
            if not first_half or (k is not None and k not in (HALF - 2, HALF - 1)):
                return None
            if s.r == 0:
                return s.half - 1
            return NCH - 1 if k == HALF - 1 else None

        @block.sync
        def _(sp):
            sp.dma_start(ws_stage, Wsmall).then_inc(s_ws, 16)
            for q, sm in enumerate(s_x):
                n = slice(q * NT // 4, (q + 1) * NT // 4)
                sp.dma_start(x[:, n, :], X.rearrange("(t p) d -> p t d", p=P)[:, n, :]).then_inc(sm, 16)
            sp.dma_start(wo[:, :], Wo).then_inc(s_small, 16)
            sp.dma_start(b1[:, :], B1).then_inc(s_small, 16)
            sp.dma_start(w_stage[:, :], W12[:, 0:WCH]).then_inc(s_wst, 16)
            sp.wait_ge(s_const, NCONST)
            zero_rows = slots_x.rearrange("(n p) c -> p n c", p=P)
            sp.dma_start(zero_rows, zeros[:, :].unsqueeze(1).to_broadcast([P, ET * SLOT // P, 2 * D])).then_inc(s_zero, 16)
            sp.wait_ge(s_post, NPOST)

            def attend(s, f, k, first_half=True):
                b, par, half = s.at(0)
                if f["p"]:
                    b2_, par2, half2 = s.at(2)
                    sp.wait_ge(s_lq, b2_ + 1)
                    if k is None or b2_ >= 2:
                        for g in range(2):
                            sp.wait_ge(s_st[par2][g], 64 * half2)
                    for side, parts in enumerate(((hi_qk, lo_qk, hi_qk), (hi_qk, hi_qk, lo_qk))):
                        for n, src in enumerate(parts):
                            dst = qk_dram[par2, side, n * DK:(n + 1) * DK, :].rearrange("d (h t) -> h d t", t=S)
                            sp.dma_start(dst, src[:, side, :]).then_inc(s_wr[par2], 16)
                    sp.wait_ge(s_cl, b2_ + 1)
                    for lo, hi in ((0, 2), (2, 3), (3, 5)):
                        sp.dma_start(ctx_dram[par2, lo * DE:hi * DE, :].rearrange("(a c) t -> c a t", c=DE), part_c[:, 0:hi - lo, :]).then_inc(s_wr[par2], 16)
                    sp.wait_ge(s_wr[par2], 144 * (half2 + 1))
                    for g in range(2):
                        if k is None or k >= 0:
                            sp.wait_ge(s_ex, 16 * b + 8 * g + 8)
                        for side in range(2):
                            st = stack[:, par2, side, 8 * g:8 * g + 8, :]
                            sp.dma_start(st[0:3 * DK], qk_dram[par2, side, :, 8 * g * S:(8 * g + 8) * S].rearrange("r (h t) -> r h t", t=S)).then_inc(s_st[par2][g], 16)
                            c = ctx_dram[par2, 2 * side * DE:(2 * side + 3) * DE]
                            sp.dma_start(st[3 * DK:ROWS], c.unsqueeze(1).to_broadcast([3 * DE, 8, S])).then_inc(s_st[par2][g], 16)
                c = chunk_of(s, k, first_half)
                if c is not None and not (isinstance(c, int) and c == NCH - 1):
                    sp.wait_ge(s_wlo, c + 1)
                    src = W12[:, (c + 1) * WCH:(c + 2) * WCH] if isinstance(c, int) else W12[:, bass.ds((c + 1) * WCH, WCH)]
                    sp.dma_start(w_stage[:, :], src).then_inc(s_wst, 16)

            attention_steps(sp, 0, attend)

            xs = slots_x.rearrange("(n s p) c -> n p s c", s=2, p=P)
            ys = slots_y.rearrange("(n s p) d -> n p s d", s=2, p=P)
            sp.wait_ge(s_scat, 16 * 2 * NT)
            sp.dma_start(b2, B2.to_broadcast([P, NE * D])).then_inc(s_b2, 16)

            def expert(quad, r, a, b, c, e, e_before):
                t = 4 * quad + r
                if a:
                    todo = [(quad + (r + 3) // 4, (r + 3) % 4)]
                    if isinstance(quad, int):
                        todo = [(n // 4, n % 4) for n in ((0, 1, 2) if t < 0 else (t + 3,)) if n < ET]
                    for q2, r2 in todo:
                        n = 4 * q2 + r2
                        if not isinstance(n, int) or n >= 4:
                            sp.wait_ge(s_ft, n - 3)
                        if isinstance(n, int):
                            src = xs[n]
                        else:
                            src = xs[bass.ds(n, 1)].rearrange("n p s c -> (n p) s c")
                        sp.dma_start(xr[r2], src).then_inc(s_xr[r2], 16)
                if c:
                    n = t - 1
                    sp.wait_ge(s_fy, n + 1)
                    dst = ys[n] if isinstance(n, int) else ys[bass.ds(n, 1)].rearrange("n p s d -> (n p) s d")
                    sp.dma_start(dst, ye[(r - 1) % 2]).then_inc(s_ys[(r - 1) % 2], 16)

            expert_steps(sp, expert)

            out_v = out.rearrange("(n s p) d -> n p s d", s=2, p=P)

            def attend_store(s, f, k):
                attend(s, f, k, False)
                if f["c"]:
                    b = s.at(-2)[0]
                    sp.wait_ge(s_c1, b - HALF + 1)
                    sp.wait_ge(s_cb, b - HALF + 1)
                    for n in (b - HALF, b):
                        if isinstance(n, int):
                            sp.dma_start(out_v[n], x[:, 2 * n:2 * n + 2, :]).then_inc(s_out, 16)
                        else:
                            sp.dma_start(out_v[bass.ds(n, 1)].rearrange("n p s d -> (n p) s d"), x[:, bass.ds(2 * n, 2), :]).then_inc(s_out, 16)

            attention_steps(sp, HALF, attend_store)
            sp.wait_ge(s_out, 16 * B)

        @block.gpsimd
        def _(pool):
            c = [0]

            def const(ins, wait=False):
                c[0] += 1
                ins.then_inc(s_const, 1)
                if wait:
                    pool.wait_ge(s_const, c[0])

            const(pool.memset(zeros[:, :], 0.0))
            const(pool.memset(ident[:, :], 0.0))
            const(pool.memset(ident16[:, :], 0.0))
            const(pool.memset(before[:, :], 1.0))
            const(pool.memset(ones16[:, :], 1.0), wait=True)
            for m in (ident, ident16):
                const(pool.affine_select(out=m[:, :], in_=m[:, :], compare_op=ALU.not_equal, fill=1.0, base=0,
                                         pattern=[[-1, P]], channel_multiplier=1))
            const(pool.affine_select(out=before[:, :], in_=before[:, :], compare_op=ALU.is_gt, fill=0.0, base=0,
                                     pattern=[[1, P]], channel_multiplier=-1))
            const(pool.iota(tile_no[:, :], pattern=[[1, ET + 4]], base=0, channel_multiplier=0))
            const(pool.memset(cnt8[:, 3, :], 0.0), wait=True)
            assert c[0] == NCONST
            for par in range(2):
                pool.memset(stack[64:ROWS + 1, par, 1, :, :], 1.0).then_inc(s_post, 1)
                pool.wait_ge(s_post, par + 1)
            pool.memset(V[:, :, :, :, :], 0.0).then_inc(s_post, 1)
            pool.wait_ge(s_post, 3)
            pool.memset(V[:, :, :, :, DK:DK + 1], 1.0).then_inc(s_post, 1)
            chain = [0]

            def link(ins):
                chain[0] += 1
                ins.then_inc(s_pd, 1)
                pool.wait_ge(s_pd, chain[0])

            def sum_experts(out_, v, into):
                link(pool.tensor_tensor(into[:, :, 0:4], v[:, :, 0:4], v[:, :, 4:8], ALU.add))
                link(pool.tensor_tensor(into[:, :, 0:2], into[:, :, 0:2], into[:, :, 2:4], ALU.add))
                link(pool.tensor_tensor(out_, into[:, :, 0], into[:, :, 1], ALU.add))

            flat = lambda v: v.rearrange("p t e -> p (t e)")
            pool.wait_ge(s_cntr, 2)
            link(pool.tensor_copy(flat(Ta), flat(scan[0])))
            pool.wait_ge(s_exp8, 1)
            sum_experts(tmp[0][:, :], Ex, Tb)
            for j in range(2):
                link(pool.tensor_tensor(Tb, Ex, sel[j], ALU.mult))
                sum_experts(prob[j][:, :], Tb, Tb)
            src, dst, d = scan[0], scan[1], 1
            while d < NT:
                link(pool.tensor_copy(dst[:, 0:d, :], src[:, 0:d, :]))
                link(pool.tensor_tensor(dst[:, d:NT, :], src[:, d:NT, :], src[:, 0:NT - d, :], ALU.add))
                src, dst, d = dst, src, 2 * d
            link(pool.tensor_scalar(cnt8[:, 0, :], src[:, NT - 1, :], SLOT / 2 - 0.5, 1 / SLOT, ALU.add, ALU.mult))
            link(pool.tensor_scalar(cnt8[:, 0, :], cnt8[:, 0, :], 2.0 ** 23, None, ALU.add))
            link(pool.tensor_scalar(cnt8[:, 0, :], cnt8[:, 0, :], -2.0 ** 23, None, ALU.add))
            link(pool.tensor_copy(cnt8[:, 1, :], cnt8[:, 0, :]))
            for e in range(1, NE):
                link(pool.tensor_tensor(cnt8[:, 1, e:e + 1], cnt8[:, 1, e - 1:e], cnt8[:, 0, e:e + 1], ALU.add))
            link(pool.tensor_tensor(cnt8[:, 2, :], cnt8[:, 1, :], cnt8[:, 0, :], ALU.subtract))
            link(pool.tensor_scalar(cnt8[:, 3, :], cnt8[:, 2, :], float(SLOT), None, ALU.mult))
            assert chain[0] == NRANK
            link(pool.tensor_tensor(dst, src, Ta, ALU.subtract))
            link(pool.tensor_tensor(Ta, before_tok, dst, ALU.add))
            link(pool.tensor_tensor(Ta, Ta, cnt8[:, 3, :].unsqueeze(1).to_broadcast([P, NT, NE]), ALU.add))
            for j in range(2):
                link(pool.tensor_tensor(Tb, Ta, sel[j], ALU.mult))
                sum_experts(tmp[2][:, :], Tb, Tb)
                link(pool.tensor_copy(pos[j][:, :], tmp[2][:, :]))
            pool.nop().then_inc(s_pos, 1)
            pool.wait_ge(s_zero, 16)
            for t in range(NT):
                for j in range(2):
                    pool.indirect_dma_start(slots_x, bass.IndirectOffsetOnAxis(pos[j][:, t:t + 1], 0), rows[:, t, :], None).then_inc(s_scat, 16)
            for par in range(2):
                pool.wait_ge(s_ys[par], 16 * (ET // 2))
            for n in range(HALF):
                if n >= 2:
                    pool.wait_ge(s_c1, n - 1)
                    pool.wait_ge(s_cb, n - 1)
                for i, b in enumerate((n, n + HALF)):
                    for q in range(2):
                        for j in range(2):
                            t = 2 * b + q
                            pool.indirect_dma_start(y_tok[n % 2][:, 4 * i + 2 * q + j, :], None, slots_y,
                                                    bass.IndirectOffsetOnAxis(pos[j][:, t:t + 1], 0)).then_inc(s_yg[n % 2], 16)
                pool.wait_ge(s_yg[n % 2], 128 * (n // 2 + 1))
                y = y_tok[n % 2].rearrange("p (b q j) d -> p b q j d", b=2, j=2)
                for i, b in enumerate((n, n + HALF)):
                    for j in range(2):
                        link(pool.tensor_tensor(y[:, i, :, j, :], y[:, i, :, j, :], prob[j][:, 2 * b:2 * b + 2].unsqueeze(2).to_broadcast([P, 2, D]), ALU.mult))
                y = y_tok[n % 2].rearrange("p (t j) d -> p t j d", j=2)
                pool.tensor_tensor(y[:, :, 0, :], y[:, :, 0, :], y[:, :, 1, :], ALU.add).then_inc(s_ysum, 1)
                pool.wait_ge(s_ysum, n + 1)

        @block.scalar
        def _(act):
            act.wait_ge(s_ws, 16)
            act.activation(ws[:, 0, :], ws_stage, ACT.Copy, scale=WS).then_inc(s_hiw, 1)
            act.wait_ge(s_small, 32)
            act.wait_ge(s_d, 1)
            act.activation(tmp[1][:, :], tmp[0][:, :], ACT.Sqrt).then_inc(s_sd, 1)

            def norm(i, a, b):
                for r in range(2):
                    if a:
                        act.wait_ge(s_rows, 2 * i + r if not isinstance(i, int) else max(2 * i + r, 1))
                        for j in range(2, 4):
                            t = 8 * i + 4 * r + j
                            ins = act.activation(xn32[r][:, j, :], x[:, bass.ds(t, 1), :].rearrange("p a d -> p (a d)"), ACT.Identity,
                                                 bias=shift[:, bass.ds(t, 1)], scale=rstd[:, bass.ds(t, 1)])
                        ins.then_inc(s_xb, 1)
                    if b:
                        act.wait_ge(s_tr, 2 * i + r - 1)
                        for part in range(2):
                            act.activation(xT[:, part, bass.ds((2 * i - 2 + r) * 4 * P, 4 * P)], bank[2 * r + part][:, :], ACT.Copy).then_inc(s_xt, 1)

            lagged(act, NT // 8, norm)

            act.wait_ge(s_post, NPOST)

            def attend(s, f, k, first_half=True):
                b, par, half = s.at(0)
                ch = chunk_of(s, k, first_half)
                for u in range(8):
                    g = u // 2
                    if f["x"]:
                        for n in (2 * u, 2 * u + 1):
                            act.wait_ge(s_ex, 16 * b + n + 1)
                            if k != 0 or u >= 2:
                                act.wait_ge(s_pv, 8 * b + u - 1)
                            act.activation(A[:, n % 4, :, :].rearrange("p h s -> p (h s)"), EX[n % 2][:, :], ACT.Exp, scale=SCALE).then_inc(s_xp, 1)
                    if u % 2 == 0 and (f["x"] if u else f["o"]):
                        bb, pp, _ = s.at(0 if u else -1)
                        gg = g - 1 if u else 3
                        act.wait_ge(s_pv, 8 * bb + 2 * gg + 2)
                        if gg == 0 and (k is None or bb >= 2):
                            act.wait_ge(s_ot, 2 * bb - 2)
                        act.activation(O[:, pp, gg, :], PV[:, 0:S], ACT.Copy).then_inc(s_pe, 1)
                    if u == 1 and f["x"]:
                        act.wait_ge(s_mt, 2 * b + 2)
                        if k is None or b >= 1:
                            act.wait_ge(s_mr[1 - par][1], 16 * (s.at(-1)[2] + 1))
                        act.activation(mT[:, 1, :, :].rearrange("h q t -> h (q t)"), MISC[1][0:8, 0:S // 2].bitcast(F16), ACT.Copy).then_inc(s_mte, 1)
                        act.wait_ge(s_mte, 2 * b + 2)
                        act.dma_start(stack[ROWS:ROWS + 1, par, 0, 8:16, :], mT[:, 1, :, :].rearrange("h q t -> h (q t)")).then_inc(s_mr[par][1], 16)
                    if u == 0 and f["p"]:
                        b2_, par2, half2 = s.at(2)
                        act.wait_ge(s_qk, b2_ + 1)
                        if k is None or b2_ >= 1:
                            act.wait_ge(s_wr[1 - par2], 144 * (s.at(1)[2] + 1))
                        act.activation(hi_qk[:, :, :].rearrange("p a t -> p (a t)"), MISC[0][:, :], ACT.Copy, scale=1 / WS).then_inc(s_hq, 1)
                    if u == 2 and f["m"]:
                        b1_, par1, _ = s.at(1)
                        act.wait_ge(s_v, b1_ + 1)
                        if f["p"]:
                            act.wait_ge(s_cx, b1_ + 2)
                        if k is None or b1_ >= 2:
                            act.wait_ge(s_pv, 8 * b1_ - 8)
                        act.activation(V[:, par1, :, :, 0:DK], MISC[0][:, S:2 * S].rearrange("p (c h d) -> p c h d", c=2, d=DK), ACT.Copy, scale=1 / WS).then_inc(s_vc, 1)
                    if u == 2 and f["p"]:
                        act.wait_ge(s_cx, b2_ + 1)
                        act.activation(part_c[:, 0, :], MISC[0][0:DE, 0:S], ACT.Copy, scale=CTX / WS).then_inc(s_ch, 1)
                    if u == 4 and f["m"]:
                        b1_, par1, _ = s.at(1)
                        act.wait_ge(s_mt, 2 * b1_ + 1)
                        if k is None or b1_ >= 1:
                            act.wait_ge(s_mr[1 - par1][0], 16 * (s.at(0)[2] + 1))
                        act.activation(mT[:, 0, :, :].rearrange("h q t -> h (q t)"), MISC[0][0:8, 0:S // 2].bitcast(F16), ACT.Copy).then_inc(s_mte, 1)
                        act.wait_ge(s_mte, 2 * b1_ + 1)
                        act.dma_start(stack[ROWS:ROWS + 1, par1, 0, 0:8, :], mT[:, 0, :, :].rearrange("h q t -> h (q t)")).then_inc(s_mr[par1][0], 16)
                    if u == 5 and ch is not None:
                        act.wait_ge(s_wst, 16 * (ch + 1))
                        dst = w12[:, 0, ch * WCH:(ch + 1) * WCH] if isinstance(ch, int) else w12[:, 0, bass.ds(ch * WCH, WCH)]
                        act.activation(dst, w_stage[:, :], ACT.Copy, scale=FS).then_inc(s_whi, 1)
                    if u == 6 and f["o"]:
                        bo = s.at(-1)[0]
                        act.wait_ge(s_oT, bo + 1)
                        if k is None or bo >= 1:
                            act.wait_ge(s_wo, bo)
                        act.activation(oT[:, :], MISC[0][:, 0:2 * P], ACT.Copy).then_inc(s_oTe, 1)
                if k == -2:
                    act.wait_ge(s_sub, 1)
                    act.activation(Ex, Ex, ACT.Exp).then_inc(s_exp8, 1)
                if k == 1:
                    act.wait_ge(s_routed, 1)
                    act.wait_ge(s_pos, 1)

            attention_steps(act, 0, attend)

            def expert(quad, r, a, b, c, e, e_before):
                if b:
                    t = 4 * quad + r
                    if not isinstance(t, int) or t >= 2:
                        act.wait_ge(s_fl, 2 * t - 2)
                    for fc in range(FC):
                        act.wait_ge(s_fu, 4 * t + fc + 1)
                        act.activation(h32[r % 2][:, fc, :], bank[fc][:, 0:SLOT], ACT.Gelu_apprx_tanh, bias=b1[:, bass.ds(e + fc, 1)], scale=1 / FS).then_inc(s_fg, 1)

            expert_steps(act, expert, expert_numbers(nc, act, tile_e[0:1, 1, :], FC))
            attention_steps(act, HALF, lambda s, f, k: attend(s, f, k, False))

        @block.vector
        def _(dve):
            chain = [0]

            def link(ins, n=1):
                chain[0] += n
                ins.then_inc(s_d, 1)
                dve.wait_ge(s_d, chain[0])

            def then(ins):
                chain[0] += 1
                ins.then_inc(s_d, 1)

            dve.wait_ge(s_hiw, 1)
            dve.scalar_tensor_tensor(out=ws[:, 1, :], in0=ws_stage, scalar=WS, in1=ws[:, 0, :], op0=ALU.mult, op1=ALU.subtract).then_inc(s_low, 1)
            for q in range(4):
                dve.wait_ge(s_x[q], 16)
                for t in range(q * NT // 4, (q + 1) * NT // 4):
                    ins = dve.bn_stats(stats[:, t, :], x[:, t, :])
                ins.then_inc(s_rd, 1)
            dve.wait_ge(s_rd, NT // 16)
            st = stats
            t0, t1, t2, t3 = (t[:, :] for t in tmp)
            for out_, a, b_, op in ((t1, st[:, :, 1], st[:, :, 4], ALU.add), (t2, st[:, :, 1], st[:, :, 4], ALU.subtract), (t3, st[:, :, 2], st[:, :, 5], ALU.add)):
                ins = dve.tensor_tensor(out_, a, b_, op)
            ins.then_inc(s_rd, 1)
            dve.wait_ge(s_rd, NT // 16 + 1)
            dve.tensor_scalar(mean[:, :], t1, 0.5, None, ALU.mult)
            dve.tensor_tensor(t2, t2, t2, ALU.mult)
            dve.tensor_scalar(t3, t3, 1.0 / D, EPS, ALU.mult, ALU.add).then_inc(s_rd, 1)
            dve.wait_ge(s_rd, NT // 16 + 2)
            link(dve.scalar_tensor_tensor(out=t0, in0=t2, scalar=0.25, in1=t3, op0=ALU.mult, op1=ALU.add))
            dve.wait_ge(s_sd, 1)
            link(dve.reciprocal(t2, t1))
            link(dve.tensor_tensor(t3, t2, t2, ALU.mult))
            link(dve.tensor_tensor(t3, t3, t0, ALU.mult))
            link(dve.tensor_scalar(t3, t3, -0.5, 1.5, ALU.mult, ALU.add))
            link(dve.tensor_tensor(rstd[:, :], t2, t3, ALU.mult))
            dve.scalar_tensor_tensor(out=shift[:, :], in0=mean[:, :], scalar=-1.0, in1=rstd[:, :], op0=ALU.mult, op1=ALU.mult).then_inc(s_rows, 1)
            c0 = chain[0]
            dve.wait_ge(s_rows, 1)
            with dve.Fori(0, NT // 8, 1) as i:
                for r in range(2):
                    if r == 1:
                        dve.wait_ge(s_rows, 2 * i + 1)
                    for j in range(2):
                        t = 8 * i + 4 * r + j
                        ins = dve.tensor_scalar(xn32[r][:, j, :], x[:, bass.ds(t, 1), :].rearrange("p a d -> p (a d)"),
                                                mean[:, bass.ds(t, 1)], rstd[:, bass.ds(t, 1)], ALU.subtract, ALU.mult)
                    ins.then_inc(s_xa, 1)
                for r in range(2):
                    dve.wait_ge(s_xa, 2 * i + r + 1)
                    dve.wait_ge(s_xb, 2 * i + r + 1)
                    dve.tensor_copy(rows[:, bass.ds(8 * i + 4 * r, 4), 0:D], xn32[r]).then_inc(s_d, 1)
                for r in range(2):
                    dve.wait_ge(s_d, 2 * i + c0 + r + 1)
                    dve.tensor_tensor(rows[:, bass.ds(8 * i + 4 * r, 4), D:2 * D], xn32[r], rows[:, bass.ds(8 * i + 4 * r, 4), 0:D], ALU.subtract).then_inc(s_rows, 1)
                dve.wait_ge(s_rows, 2 * i + 2)
            chain[0] += 2 * (NT // 8)
            flat = lambda v: v.rearrange("p t e -> p (t e)")
            def rank():
                dve.wait_ge(s_gate, NT // 4)
                link(dve.tensor_scalar(flat(L), bank[4][:, :], 1 / WS, None, ALU.mult))
                for e in range(NE):
                    won = wins[:, e, :].rearrange("p (t e) -> p t e", e=NE)
                    then(dve.tensor_tensor(won[:, :, 0:e + 1], L[:, :, e:e + 1].to_broadcast([P, NT, e + 1]), L[:, :, 0:e + 1], ALU.is_gt))
                    if e < NE - 1:
                        then(dve.tensor_tensor(won[:, :, e + 1:NE], L[:, :, e:e + 1].to_broadcast([P, NT, NE - 1 - e]), L[:, :, e + 1:NE], ALU.is_ge))
                then(dve.tensor_reduce(tmp[0][:, :], L, AX.X, ALU.max))
                dve.wait_ge(s_d, chain[0])
                dve.tensor_tensor(Ex, L, tmp[0][:, :].unsqueeze(2).to_broadcast([P, NT, NE]), ALU.subtract).then_inc(s_sub, 1)
                n = NE
                while n > 2:
                    n //= 2
                    link(dve.tensor_tensor(wins[:, 0:n, :], wins[:, 0:n, :], wins[:, n:2 * n, :], ALU.add))
                link(dve.tensor_tensor(flat(Ta), wins[:, 0, :], wins[:, 1, :], ALU.add))
                dve.tensor_scalar(picked[:, :], flat(Ta), 2.0, None, ALU.is_lt).then_inc(s_m, 1)
                for j in range(2):
                    link(dve.tensor_scalar(flat(sel[j]), flat(Ta), float(j), None, ALU.is_equal))

            def counts():
                dve.wait_ge(s_cnt, 1)
                dve.tensor_copy(flat(scan[0]), bank[4][:, :]).then_inc(s_cntr, 1)
                dve.tensor_copy(flat(before_tok), bank[5][:, :]).then_inc(s_cntr, 1)

            def table():
                dve.wait_ge(s_pd, NRANK)
                link(dve.reciprocal(tmp[1][:, :], tmp[0][:, :]))
                for j in range(2):
                    then(dve.tensor_tensor(prob[j][:, :], prob[j][:, :], tmp[1][:, :], ALU.mult))
                n = ET + 4
                tf = tile_f[:, 0:n * NE].rearrange("p (t e) -> p t e", e=NE)
                te = tile_f[:, n * NE:n * NE + n].rearrange("p (q j) -> p q j", j=4)
                word = tile_f[:, n * (NE + 1):]
                link(dve.tensor_copy(tf, tile_no[:, :].unsqueeze(2).to_broadcast([1, n, NE])))
                yield
                link(dve.tensor_tensor(tf, tf, cnt8[0:1, 1, :].unsqueeze(1).to_broadcast([1, n, NE]), ALU.is_ge))
                yield
                link(dve.tensor_reduce(te.rearrange("p q j -> p (q j)"), tf, AX.X, ALU.add))
                link(dve.tensor_scalar(te, te, float(NE - 1), None, ALU.min))
                yield
                acc = te[:, 1:1 + ET // 4, 0]
                for j in (3, 2, 1, 0):
                    link(dve.scalar_tensor_tensor(out=word, in0=acc, scalar=float(2 ** DIGIT), in1=te[:, 0:ET // 4, j], op0=ALU.mult, op1=ALU.add))
                    acc = word
                link(dve.tensor_scalar(tile_e[:, 0, :], word, float(FF), None, ALU.mult))
                dve.tensor_scalar(tile_e[:, 1, :], word, float(FC), None, ALU.mult).then_inc(s_routed, 1)

            pieces = table()
            c_rd = NT // 16 + 2

            def combine(s, i):
                bc, par, half = s.at(-2)
                if i == 0:
                    dve.wait_ge(s_ysum, bc - HALF + 1)
                else:
                    dve.wait_ge(s_acc, bc + 1)
                t = 2 * (bc - HALF * (1 - i))
                xs_ = x[:, t:t + 2, :] if isinstance(t, int) else x[:, bass.ds(t, 2), :]
                y = y_tok[par].rearrange("p (b q j) d -> p b q j d", b=2, j=2)[:, i, :, 0, :]
                dve.tensor_tensor(xs_, xs_, y, ALU.add).then_inc((s_c1, s_cb)[i], 1)

            def attend(s, f, k, first_half=True):
                b, par, half = s.at(0)
                b1_, par1, half1 = s.at(1)
                ch = chunk_of(s, k, first_half)
                for u in range(8):
                    if first_half and k == -2 and u == 3:
                        rank()
                    if first_half and k == -1 and u == 0:
                        counts()
                    if first_half and k == 1 and u in (3, 4, 5, 6):
                        next(pieces, None)
                    if f["m"]:
                        g, qt = u // 2, u % 2
                        for p in range(2):
                            n = 2 * u + p
                            dve.wait_ge(s_mx, 16 * b1_ + n + 1)
                            dve.tensor_reduce(mx[:, par1, qt, 4 * g + 2 * p:4 * g + 2 * p + 2], MX[MX_ORDER[n]][:, :].rearrange("q (h k) -> q h k", h=2), AX.X, ALU.max).then_inc(s_red, 1)
                        if u in (3, 7):
                            a = u // 4
                            dve.wait_ge(s_red, 16 * b1_ + 8 * a + 8)
                            if k is None or b1_ >= 1:
                                dve.wait_ge(s_mt, 2 * b1_ + a - 1)
                            dve.tensor_scalar(negm[:, a, :, :], mx[:, par1, :, 8 * a:8 * a + 8], -1.0, None, ALU.mult).then_inc(s_nm, 1)
                    if u == 0 and f["c"]:
                        bc = s.at(-2)[0]
                        dve.wait_ge(s_wo, bc + 1)
                        xs_ = x[:, 2 * bc:2 * bc + 2, :] if isinstance(bc, int) else x[:, bass.ds(2 * bc, 2), :]
                        dve.tensor_tensor(xs_, xs_, MISC[1][:, 0:2 * P].rearrange("p (q d) -> p q d", q=2), ALU.add).then_inc(s_acc, 1)
                    if u == 0 and f["c"] and not first_half:
                        combine(s, 0)
                        combine(s, 1)
                    if u == 0 and f["p"]:
                        b2_ = s.at(2)[0]
                        dve.wait_ge(s_hq, b2_ + 1)
                        dve.scalar_tensor_tensor(out=lo_qk[:, :, :].rearrange("p a t -> p (a t)"), in0=MISC[0][:, :], scalar=1 / WS,
                                                 in1=hi_qk[:, :, :].rearrange("p a t -> p (a t)"), op0=ALU.mult, op1=ALU.subtract).then_inc(s_lq, 1)
                    if u == 2 and f["p"]:
                        dve.wait_ge(s_ch, b2_ + 1)
                        dve.scalar_tensor_tensor(out=part_c[:, 1, :], in0=MISC[0][0:DE, 0:S], scalar=CTX / WS, in1=part_c[:, 0, :],
                                                 op0=ALU.mult, op1=ALU.subtract).then_inc(s_cl, 1)
                    if u in (3, 5) and f["o"]:
                        bo = s.at(-1)[0]
                        qt = (u - 3) // 2
                        dve.wait_ge(s_ot, 2 * bo + qt + 1)
                        v = MISC[1][:, :].rearrange("q (h r) -> q h r", r=32)
                        dve.reciprocal(rden[:, qt, :], v[:, :, DK]).then_inc(s_rd, 1)
                        dve.wait_ge(s_rd, 2 * bo + qt + 1 + c_rd)
                        if qt == 0 and (k is None or bo >= 1):
                            dve.wait_ge(s_oT, bo)
                        dve.tensor_tensor(o_n[:, qt, :, :], v[:, :, 0:DK], rden[:, qt, :].unsqueeze(2).to_broadcast([P, H, DK]), ALU.mult).then_inc(s_on, 1)
                    if u == 6 and ch is not None:
                        dve.wait_ge(s_whi, ch + 1)
                        hi, lo = ((w12[:, part, ch * WCH:(ch + 1) * WCH] if isinstance(ch, int) else w12[:, part, bass.ds(ch * WCH, WCH)]) for part in range(2))
                        dve.scalar_tensor_tensor(out=lo, in0=w_stage[:, :], scalar=FS, in1=hi, op0=ALU.mult, op1=ALU.subtract).then_inc(s_wlo, 1)

            attention_steps(dve, 0, attend)
            assert next(pieces, None) is None
            dve.wait_ge(s_b2, 16)

            def expert(quad, r, a, b, c, e, e_before):
                t = 4 * quad + r
                static = isinstance(t, int)
                if a:
                    n, par = t + 1, (r + 1) % 2
                    dve.wait_ge(s_ft, n + 1)
                    if not static or n >= 2:
                        dve.wait_ge(s_fu, 4 * n - 4)
                    dve.tensor_copy(xt[par].rearrange("p a s -> p (a s)"), bank[4 + par][:, 0:SLOT].bitcast(F16)).then_inc(s_fx, 1)
                if b:
                    par = r % 2
                    for hf in range(2):
                        dve.wait_ge(s_fg, 4 * t + 2 * hf + 2)
                        if hf == 0 and (not static or t >= 2):
                            dve.wait_ge(s_fd, t - 1)
                        hi, lo, h = (v[:, 2 * hf:2 * hf + 2, :] for v in (hp[par][:, 0], hp[par][:, 1], h32[par]))
                        dve.tensor_copy(hi, h).then_inc(s_fh, 1)
                        dve.wait_ge(s_fh, 2 * t + hf + 1)
                        dve.tensor_tensor(lo, h, hi, ALU.subtract).then_inc(s_fl, 1)
                if c:
                    n, par = t - 1, (r - 1) % 2
                    dve.wait_ge(s_fd, n + 1)
                    if not static or n >= 2:
                        dve.wait_ge(s_ys[par], 16 * (2 * quad + (r - 1) // 2))
                    dve.scalar_tensor_tensor(out=ye[par], in0=bank[6 + par][:, 0:2 * D].rearrange("p (s d) -> p s d", s=2), scalar=1 / FS,
                                             in1=b2[:, bass.ds(e_before * (D // FC), D)].unsqueeze(1).to_broadcast([P, 2, D]), op0=ALU.mult, op1=ALU.add).then_inc(s_fy, 1)

            expert_steps(dve, expert, expert_numbers(nc, dve, tile_e[0:1, 1, :], FC))

            attention_steps(dve, HALF, lambda s, f, k: attend(s, f, k, False))

        @block.tensor
        def _(pe):
            pe.wait_ge(s_const, NCONST)
            pe.wait_ge(s_low, 1)

            def norm(i, a, b):
                if a:
                    for r in range(2):
                        pe.wait_ge(s_rows, 2 * i + r + 2)
                        if not isinstance(i, int):
                            pe.wait_ge(s_xt, 4 * i + 2 * r - 2)
                        for part in range(2):
                            for j in range(4):
                                t = 8 * i + 4 * r + j
                                mm = pe.matmul(bank[2 * r + part][:, j * P:(j + 1) * P], rows[:, bass.ds(t, 1), part * D:(part + 1) * D].rearrange("p a d -> p (a d)"),
                                               ident16[:, :], start=True, stop=True)
                        mm.then_inc(s_tr, 1)
                if b:
                    tok, log = ((i - 1) * 8 * n if isinstance(i, int) else pe.snap((i - 1) * 8 * n) for n in (P, NE))
                    for r in range(2):
                        pe.wait_ge(s_xt, 4 * i + 2 * r - 2)
                        for j in range(4):
                            t = 4 * r + j
                            for n, (pa, pb) in enumerate(TERMS):
                                mm = pe.matmul(bank[4][:, bass.ds(log + t * NE, NE)], xT[:, pa, bass.ds(tok + t * P, P)], ws[:, pb, CG:CG + NE], start=(n == 0), stop=(n == 2))
                        mm.then_inc(s_gate, 1)

            lagged(pe, NT // 8, norm, end=False)

            def drained(e, s, f, k):
                def readers(e, off, f, k):
                    n = lambda o: s.at(off + o)[0]
                    return {0: f["p"] and [(s_lq, n(2) + 1)], 1: f["x"] and [(s_mte, 2 * n(0) + 2)],
                            2: (f["p"] or f["m"]) and [(s_cl, n(2) + 1)] * f["p"] + [(s_vc, n(1) + 1)] * f["m"],
                            3: f["o"] and [(s_on, 2 * n(-1) + 1)], 4: f["m"] and [(s_mte, 2 * n(1) + 1)],
                            5: f["o"] and [(s_on, 2 * n(-1) + 2)], 6: f["o"] and [(s_oTe, n(-1) + 1)],
                            7: f["o"] and [(s_acc, n(-1) + 1)]}[e]
                off, ee = 0, e - 2
                while True:
                    if ee < 0:
                        ee += 8
                        off -= 1
                        if k is not None:
                            if off < -2:
                                return
                            f = attention_flags(k + off, HALF * phase[0])
                    got = readers(ee, off, f, k)
                    if got:
                        for sm, v in got:
                            if not isinstance(v, int) or v > 0:
                                pe.wait_ge(sm, v)
                        return
                    ee -= 2

            phase = [0]

            def xcols(part, b, n=S, o=0):
                return xT[:, part, b * S + o:b * S + o + n] if isinstance(b, int) else xT[:, part, bass.ds(b * S + o, n)]

            def attend(s, f, k):
                b, par, half = s.at(0)
                b1_, par1, half1 = s.at(1)
                b2_ = s.at(2)[0]
                bo, paro, _ = s.at(-1)

                def values(bb, pp, v):
                    g, c = v // 2, v % 2
                    pe.wait_ge(s_xp, 16 * bb + 2 * v + 2)
                    if v == 0:
                        pe.wait_ge(s_vc, bb + 1)
                    if c == 0 and (not isinstance(bb, int) or 4 * bb + g >= 1):
                        pe.wait_ge(s_pe, 4 * bb + g)
                    for i in range(4):
                        mm = pe.matmul(PV[32 * i:32 * i + 32, 0:S], V[:, pp, c, 4 * g + i, :], A[:, (2 * v + i // 2) % 4, i % 2, :],
                                       start=(c == 0), stop=(c == 1))
                    mm.then_inc(s_pv, 1)

                if k == -1:
                    pe.wait_ge(s_cntr, 2)
                for u in range(8):
                    g, c = u // 2, u % 2
                    def shifted(p):
                        n = 2 * u + p
                        if p == 0 and u in (0, 4):
                            pe.wait_ge(s_mr[par][u // 4], 16 * (half + 1))
                        if not isinstance(b, int) or 16 * b + n >= 2:
                            pe.wait_ge(s_xp, 16 * b + n - 1)
                        for i in range(2):
                            h = 4 * g + 2 * p + i
                            mm = pe.matmul(EX[p][:, i * S:(i + 1) * S], stack[0:ROWS + 1, par, 1, h, c * P:(c + 1) * P], stack[0:ROWS + 1, par, 0, h, :], start=True, stop=True)
                        mm.then_inc(s_ex, 1)

                    def plain(p):
                        n = 2 * u + p
                        if p == 0 and u in (0, 4):
                            pe.wait_ge(s_st[par1][g // 2], 64 * (half1 + 1))
                        if not isinstance(b1_, int) or 16 * b1_ + mx_read(n) > 0:
                            pe.wait_ge(s_red, 16 * b1_ + mx_read(n))
                        for i in range(2):
                            h = 4 * g + 2 * p + i
                            mm = pe.matmul(MX[MX_ORDER[n]][:, i * S:(i + 1) * S], stack[0:ROWS, par1, 0, h, c * P:(c + 1) * P], stack[0:ROWS, par1, 1, h, :], start=True, stop=True)
                        mm.then_inc(s_mx, 1)

                    if f["m"]:
                        plain(0)
                    if f["x"]:
                        shifted(0)
                    if f["m"]:
                        plain(1)
                    if f["x"]:
                        shifted(1)
                    if u == 0 and f["o"]:
                        values(bo, paro, 7)
                    if u > 0 and f["x"]:
                        values(b, par, u - 1)
                    M = MISC[u % 2]
                    if (u == 1 and f["x"]) or (u == 4 and f["m"]):
                        a = 1 if u == 1 else 0
                        drained(u, s, f, k)
                        pe.wait_ge(s_nm, 2 * (b if u == 1 else b1_) + a + 1)
                        for q in range(2):
                            mm = pe.transpose(M[0:8, 0:S // 2].bitcast(F16)[:, q * P:(q + 1) * P], negm[:, a, q, :], ident16[:, :])
                        mm.then_inc(s_mt, 1)
                    if u == 0 and k == HALF and phase[0] == 1:
                        pe.wait_ge(s_fy, ET)
                    if u == 0 and f["p"]:
                        drained(u, s, f, k)
                        for side, col in ((0, CQ), (1, CK)):
                            for n, (pa, pb) in enumerate(TERMS):
                                mm = pe.matmul(M[:, side * S:(side + 1) * S], ws[:, pa, col:col + D], xcols(pb, b2_), start=(n == 0), stop=(n == 2))
                        mm.then_inc(s_qk, 1)
                    if u == 2 and (f["p"] or f["m"]):
                        drained(u, s, f, k)
                        if f["m"]:
                            for q in range(2):
                                for n, (pa, pb) in enumerate(TERMS):
                                    mm = pe.matmul(M[:, S + q * P:S + (q + 1) * P], xcols(pa, b1_, P, q * P), ws[:, pb, CV:CV + D], start=(n == 0), stop=(n == 2))
                            mm.then_inc(s_v, 1)
                        if f["p"]:
                            for n, (pa, pb) in enumerate(TERMS):
                                mm = pe.matmul(M[0:DE, 0:S], ws[:, pa, CE:CE + DE], xcols(pb, b2_), start=(n == 0), stop=(n == 2))
                            mm.then_inc(s_cx, 1)
                    if u in (3, 5) and f["o"]:
                        drained(u, s, f, k)
                        qt = (u - 3) // 2
                        if qt == 0:
                            pe.wait_ge(s_pe, 4 * bo + 4)
                        for gg in range(4):
                            mm = pe.transpose(M[:, gg * P:(gg + 1) * P], O[:, paro, gg, qt * P:(qt + 1) * P], ident[:, :])
                        mm.then_inc(s_ot, 1)
                    if u == 6 and f["o"]:
                        drained(u, s, f, k)
                        pe.wait_ge(s_on, 2 * bo + 2)
                        for q in range(2):
                            mm = pe.transpose(M[:, q * P:(q + 1) * P], o_n[:, q, :, :].rearrange("p h d -> p (h d)"), ident[:, :])
                        mm.then_inc(s_oT, 1)
                    if u == 7 and f["o"]:
                        drained(u, s, f, k)
                        pe.wait_ge(s_oTe, bo + 1)
                        for q in range(2):
                            mm = pe.matmul(M[:, q * P:(q + 1) * P], oT[:, q * P:(q + 1) * P], wo[:, :], start=True, stop=True)
                        mm.then_inc(s_wo, 1)
                if k == -2:
                    norm(NT // 8, False, True)
                    pe.wait_ge(s_m, 1)
                    pe.matmul(bank[5][:, :], before[:, :], picked[:, :], start=True, stop=True)
                    pe.matmul(bank[4][:, :], ones16[:, :], picked[:, :], start=True, stop=True).then_inc(s_cnt, 1)
            attention_steps(pe, 0, attend)
            for sm, n in ((s_red, 16 * (HALF + 1)), (s_xp, 16 * HALF), (s_pe, 4 * HALF), (s_vc, HALF + 1), (s_lq, HALF + 2), (s_cl, HALF + 2), (s_oTe, HALF), (s_acc, HALF), (s_wlo, NCH), (s_routed, 1)):
                pe.wait_ge(sm, n)

            def expert(quad, r, a, b, c, e, e_before):
                t = 4 * quad + r
                static = isinstance(t, int)
                if a:
                    n, par, r4 = t + 1, (r + 1) % 2, (r + 1) % 4
                    pe.wait_ge(s_xr[r4], 16 * (quad + (r + 1) // 4 + 1))
                    if not static or n >= 2:
                        pe.wait_ge(s_fx, n - 1)
                    v = bank[4 + par][:, 0:SLOT].bitcast(F16)
                    for part in range(2):
                        for h in range(2):
                            mm = pe.transpose(v[:, part * SLOT + h * P:part * SLOT + (h + 1) * P], xr[r4][:, h, part * D:(part + 1) * D], ident16[:, :])
                    mm.then_inc(s_ft, 1)
                if b:
                    pe.wait_ge(s_fx, t + 1)
                    for fc in range(FC):
                        if not static or t >= 1:
                            pe.wait_ge(s_fg, 4 * t + fc - 3)
                        for n, (pa, pb) in enumerate(TERMS):
                            mm = pe.matmul(bank[fc][:, 0:SLOT], w1[:, pa, bass.ds(e + fc * P, P)], xt[r % 2][:, pb, :], start=(n == 0), stop=(n == 2))
                        mm.then_inc(s_fu, 1)
                if c:
                    n, par = t - 1, (r - 1) % 2
                    pe.wait_ge(s_fl, 2 * n + 2)
                    if not static or n >= 2:
                        pe.wait_ge(s_fy, n - 1)
                    for h in range(2):
                        for fc in range(FC):
                            for m, (pa, pb) in enumerate(TERMS):
                                mm = pe.matmul(bank[6 + par][:, h * D:(h + 1) * D], hp[par][:, pa, fc, h * P:(h + 1) * P], w2[:, pb, bass.ds(e_before + fc * P, P)],
                                               start=(fc == 0 and m == 0), stop=(fc == FC - 1 and m == 2))
                    mm.then_inc(s_fd, 1)

            expert_steps(pe, expert, expert_numbers(nc, pe, tile_e[0:1, 0, :], FF))
            for sm, n in ((s_fg, FC * ET), (s_fx, ET)):
                pe.wait_ge(sm, n)
            phase[0] = 1
            attention_steps(pe, HALF, attend)


def kernel(L0_attn_X, L0_attn_Wq, L0_attn_Wk, L0_attn_Wv, L0_attn_Wo, L0_attn_We, L0_ffn_gate_w, L0_ffn_w1, L0_ffn_b1, L0_ffn_w2, L0_ffn_b2):
    import numpy as np
    import concourse.bacc as bacc
    from concourse.bass_utils import run_bass_kernel_spmd

    turned = [np.asarray(w).T for w in (L0_attn_Wq, L0_attn_Wk, L0_attn_Wv, L0_attn_We, L0_ffn_gate_w)]
    w2 = np.asarray(L0_ffn_w2).transpose(1, 2, 0).reshape(NE, FC, P, D).transpose(2, 0, 1, 3).reshape(P, NE * FF)
    w1 = np.asarray(L0_ffn_w1).transpose(2, 1, 0).reshape(D, NE * FF)
    arrays = {
        "x": np.asarray(L0_attn_X).reshape(B * S, D),
        "wsmall": np.concatenate(turned, axis=1),
        "wo": np.asarray(L0_attn_Wo).T,
        "w12": np.concatenate([w1, w2], axis=1),
        "b1": np.asarray(L0_ffn_b1).reshape(NE * FC, P).T,
        "b2": np.asarray(L0_ffn_b2).reshape(1, NE * D),
    }
    arrays = {f"in_{n}": np.ascontiguousarray(a) for n, a in arrays.items()}
    nc = bacc.Bacc("TRN2", target_bir_lowering=False, num_devices=1)
    ins = [nc.dram_tensor(n, list(a.shape), mybir.dt.from_np(a.dtype), kind="ExternalInput").ap() for n, a in arrays.items()]
    out = nc.dram_tensor("out_rows", [B * S, D], F32, kind="ExternalOutput").ap()
    build(nc, *ins, out)
    r = run_bass_kernel_spmd(nc, [arrays], core_ids=[0])
    return np.asarray(r.results[0]["out_rows"]).reshape(B, S, D)
```
